# Optimizing a Trainium2 kernel written in Bass

```python
import numpy as np
import jax
import jax.numpy as jnp

def _softmax(x, axis=-1):
    return jax.nn.softmax(x, axis=axis)

def _gelu(x):
    return jax.nn.gelu(x, approximate=True)

def _silu(x):
    return jax.nn.silu(x)

def _sigmoid(x):
    return jax.nn.sigmoid(x)

def _layernorm(x, axis=-1, eps=1e-05):
    m = jnp.mean(x, axis=axis, keepdims=True)
    v = jnp.var(x, axis=axis, keepdims=True)
    return (x - m) / jnp.sqrt(v + eps)

def _scatter_add(tgt, idx, src, axis=0):
    return tgt.at[idx].add(src)

def _segment_sum(src, seg, n):
    return jax.ops.segment_sum(src, seg, n)
kernel_name = 'mk_gnn_ffn_d1_gnn_r16_15f1ed'

def setup_inputs(seed: int=0):
    np.random.seed(seed)
    _w = jnp.asarray

    def _rec_inputs():
        import jax
        import jax.numpy as jnp
        _gk = jax.random.key(seed)
        x = -0.0003713 + 1 * jax.random.normal(jax.random.fold_in(_gk, 1), (3125, 256), jnp.float32)
        src = jax.random.randint(jax.random.fold_in(_gk, 2), (50000,), 0, 3125, jnp.int32)
        dst = jnp.minimum((3125 * jax.random.uniform(jax.random.fold_in(_gk, 3), (50000,)) ** 2.0).astype(jnp.int32), 49999)
        _o = jnp.argsort(dst, stable=True)
        src = src[_o]
        dst = dst[_o]
        return (x, src, dst)
    x, src, dst = _rec_inputs()

    def _L0_gnn_setup():
        import jax, jax.numpy as jnp
        import numpy as np
        N = 3125
        E = 12500
        H = 8
        C = 256
        IN = 256
        NEG_SLOPE = 0.2
        EPS = 1e-16
        key = jax.random.key(seed)
        k1, k2, k3, k4, k5, k6 = jax.random.split(key, 6)
        glorot = lambda k, shape, fan: jax.random.normal(k, shape, jnp.float32) * np.sqrt(2.0 / fan)
        x = jax.random.normal(k1, (N, IN), jnp.float32)
        edge_index = jax.random.randint(k2, (2, E), 0, N, jnp.int32)
        W = glorot(k3, (IN, H * C), IN + H * C)
        att_src = glorot(k4, (H, C), C)
        att_dst = glorot(k5, (H, C), C)
        bias = jnp.zeros((C,), jnp.float32)
        return {'x': x, 'edge_index': edge_index, 'W': W, 'att_src': att_src, 'att_dst': att_dst, 'bias': bias}
    _L0_gnn_all = _L0_gnn_setup()
    _L0_gnn_in = {k: v for k, v in _L0_gnn_all.items() if k in ('W', 'att_src', 'att_dst', 'bias')}
    del _L0_gnn_all

    def _L0_ffn_setup():
        import jax, jax.numpy as jnp
        import numpy as np
        NUM_EXPERTS = 8
        TOP_K = 2
        B, S, D = (8, 512, 256)

        def _moe(tokens, router_w, w1, b1, w2, b2):
            N = tokens.shape[0]
            E = router_w.shape[0]
            logits = tokens.astype(jnp.float32) @ router_w.astype(jnp.float32).T
            probs = jax.nn.softmax(logits, axis=-1)
            rw, re = jax.lax.top_k(probs, TOP_K)
            if TOP_K > 1:
                rw = rw / jnp.maximum(rw.sum(-1, keepdims=True), 1e-12)
            rw = rw.astype(tokens.dtype)
            combine = jnp.zeros((N, E), tokens.dtype).at[jnp.arange(N)[:, None], re].set(rw)
            out = tokens
            for e in range(E):
                h = jax.nn.gelu(tokens @ w1[e] + b1[e], approximate=False)
                y = h @ w2[e] + b2[e]
                out = out + combine[:, e:e + 1] * y
            return out
        key = jax.random.key(seed)
        ks = jax.random.split(key, 4)
        scale = 1.0 / np.sqrt(D).astype(np.float32)
        return {'input_embeddings': jax.random.normal(ks[0], (B, S, D), jnp.float32), 'router_w': jax.random.normal(ks[1], (NUM_EXPERTS, D), jnp.float32) * scale, 'w1': jax.random.normal(ks[2], (NUM_EXPERTS, D, D), jnp.float32) * scale, 'b1': jnp.zeros((NUM_EXPERTS, D), jnp.float32), 'w2': jax.random.normal(ks[3], (NUM_EXPERTS, D, D), jnp.float32) * scale, 'b2': jnp.zeros((NUM_EXPERTS, D), jnp.float32)}
    _L0_ffn_all = _L0_ffn_setup()
    _L0_ffn_in = {k: v for k, v in _L0_ffn_all.items() if k in ('router_w', 'w1', 'b1', 'w2', 'b2')}
    del _L0_ffn_all
    return {'x': x, 'src': src, 'dst': dst, 'L0_gnn_W': _L0_gnn_in['W'], 'L0_gnn_att_src': _L0_gnn_in['att_src'], 'L0_gnn_att_dst': _L0_gnn_in['att_dst'], 'L0_gnn_bias': _L0_gnn_in['bias'], 'L0_ffn_router_w': _L0_ffn_in['router_w'], 'L0_ffn_w1': _L0_ffn_in['w1'], 'L0_ffn_b1': _L0_ffn_in['b1'], 'L0_ffn_w2': _L0_ffn_in['w2'], 'L0_ffn_b2': _L0_ffn_in['b2']}

def reference(x, src, dst, L0_gnn_W, L0_gnn_att_src, L0_gnn_att_dst, L0_gnn_bias, L0_ffn_router_w, L0_ffn_w1, L0_ffn_b1, L0_ffn_w2, L0_ffn_b2):
    import jax
    import jax.numpy as jnp

    def _L0_gnn_ref(x, edge_index, W, att_src, att_dst, bias):
        import jax, jax.numpy as jnp
        import numpy as np
        N = 3125
        E = 12500
        H = 8
        C = 256
        IN = 256
        NEG_SLOPE = 0.2
        EPS = 1e-16
        h = (x @ W).reshape(N, H, C)
        a_src = jnp.einsum('nhc,hc->nh', h, att_src)
        a_dst = jnp.einsum('nhc,hc->nh', h, att_dst)
        src, dst = (edge_index[0], edge_index[1])
        e = jax.nn.leaky_relu(a_src[src] + a_dst[dst], NEG_SLOPE)
        m = jax.ops.segment_max(e, dst, num_segments=N)
        e = jnp.exp(e - m[dst])
        denom = jax.ops.segment_sum(e, dst, num_segments=N)
        alpha = e / (denom[dst] + EPS)
        msg = h[src] * alpha[:, :, None]
        out = jax.ops.segment_sum(msg, dst, num_segments=N)
        return out.mean(axis=1) + bias

    def _L0_ffn_ref(input_embeddings, router_w, w1, b1, w2, b2):
        import jax, jax.numpy as jnp
        import numpy as np
        NUM_EXPERTS = 8
        TOP_K = 2
        B, S, D = (8, 512, 256)

        def _moe(tokens, router_w, w1, b1, w2, b2):
            N = tokens.shape[0]
            E = router_w.shape[0]
            logits = tokens.astype(jnp.float32) @ router_w.astype(jnp.float32).T
            probs = jax.nn.softmax(logits, axis=-1)
            rw, re = jax.lax.top_k(probs, TOP_K)
            if TOP_K > 1:
                rw = rw / jnp.maximum(rw.sum(-1, keepdims=True), 1e-12)
            rw = rw.astype(tokens.dtype)
            combine = jnp.zeros((N, E), tokens.dtype).at[jnp.arange(N)[:, None], re].set(rw)
            out = tokens
            for e in range(E):
                h = jax.nn.gelu(tokens @ w1[e] + b1[e], approximate=False)
                y = h @ w2[e] + b2[e]
                out = out + combine[:, e:e + 1] * y
            return out
        b, s, d = input_embeddings.shape
        tokens = input_embeddings.reshape(b * s, d)
        return _moe(tokens, router_w, w1, b1, w2, b2).reshape(b, s, d)
    edge_index = jnp.stack([src, dst])
    x = x + _L0_gnn_ref(_layernorm(x, axis=-1), edge_index, L0_gnn_W, L0_gnn_att_src, L0_gnn_att_dst, L0_gnn_bias)
    x = x + _L0_ffn_ref(_layernorm(x, axis=-1)[None], L0_ffn_router_w, L0_ffn_w1, L0_ffn_b1, L0_ffn_w2, L0_ffn_b2)[0]
    return x

_drawn_inputs = setup_inputs


def setup_inputs(seed=0):
    import zlib

    import numpy as np

    out = dict(_drawn_inputs(seed))
    spreads = {'L0_gnn_bias': (0.0, 0.1), 'L0_ffn_b1': (0.0, 0.327), 'L0_ffn_b2': (0.0, 0.1)}
    factors = {'L0_gnn_att_dst': 3.394}
    for name, (base, spread) in spreads.items():
        noise = np.random.default_rng([zlib.crc32(name.encode()), seed]).standard_normal(out[name].shape)
        drawn = base * np.exp(spread * noise) if base else spread * noise
        out[name] = jnp.asarray(drawn.astype(out[name].dtype))
    for name, factor in factors.items():
        out[name] = (out[name] * factor).astype(out[name].dtype)
    return out
```

```python
from contextlib import ExitStack

import concourse.bass as bass
from concourse import mybir

F32 = mybir.dt.float32
I32 = mybir.dt.int32
U32 = mybir.dt.uint32
ALU = mybir.AluOpType
ACT = mybir.ActivationFunctionType
AX_X = mybir.AxisListType.X

P = 128
BIG = 1e30
LN_EPS = 1e-5
SOFTMAX_EPS = 1e-16
NEG_SLOPE = 0.2
RSQRT_MAGIC = float(0x5F3759DF)
NEWTON_STEPS = 4
INV_SQRT_LINKS = 4 + 3 * NEWTON_STEPS
CHUNKS = 16
WINDOW = 16
WIN_PER_TILE = P // WINDOW
G_RING = 16
IDX_GROUP = 4
A_RING = 8
ACC_RING = 4
UNROLL = 5


def gat_moe_kernel(nc, x, src, dst, W, att_src, att_dst, gnn_bias, router_w, w1, b1, w2, b2, out):
    N, D = x.shape
    E = src.shape[0]
    H, C = att_src.shape
    NX = router_w.shape[0]
    TILES = -(-N // P)
    FULL = N // P
    LAST = N - FULL * P
    EC = E // CHUNKS
    BLK = P - 3
    KB = EC // BLK
    NB = E // BLK
    NW = TILES * WIN_PER_TILE
    assert EC * CHUNKS == E and KB * BLK == EC and H * CHUNKS == P and H * WINDOW == P
    assert D == 2 * P and C == D and NB % G_RING == 0 and TILES % UNROLL == 0 and KB % UNROLL == 0
    assert TILES % 2 == 1 and WIN_PER_TILE % ACC_RING == 0

    xn_table = nc.dram_tensor("xn_table", [TILES * P, D], F32).ap()
    score_src_table = nc.dram_tensor("score_src_table", [TILES * P, H], F32).ap()
    score_dst_table = nc.dram_tensor("score_dst_table", [TILES * P, H], F32).ap()
    agg_table = nc.dram_tensor("agg_table", [TILES, P, 2 * H * P], F32).ap()

    with ExitStack() as ctx:
        def sb(name, shape, dt=F32):
            return ctx.enter_context(nc.sbuf_tensor(name, shape, dt))

        def sem(name):
            return ctx.enter_context(nc.semaphore(name))

        x_all = sb("x_all", [P, TILES, D])
        W_sb = sb("W_sb", [P, 2, H * C])
        w1_sb = sb("w1_sb", [P, NX, 2, D])
        w2_sb = sb("w2_sb", [P, NX, 2, D])
        alpha = sb("alpha", [BLK, NB, H])
        dst_f = sb("dst_f", [BLK, NB])
        src_b = sb("src_b", [BLK, NB], I32)
        idx_k = sb("idx_k", [BLK, KB, 2 * CHUNKS], I32)
        node_ids = sb("node_ids", [P, NW * WINDOW])
        ident = sb("ident", [P, P])
        win_end = sb("win_end", [1, NB + 1], I32)
        bias_bc = sb("bias_bc", [P, D])
        router_sb = sb("router_sb", [P, 2, NX])
        b1_sb = sb("b1_sb", [P, NX, 2])
        b2_sb = sb("b2_sb", [NX, D])
        va = sb("va", [P, 2, 2 * H])
        expert_ids = sb("expert_ids", [P, NX])
        expert_ids_i = sb("expert_ids_i", [P, NX], I32)

        zeros = sb("zeros", [P, D])

        SC = EC + 2
        work = sb("work", [P, 5 * SC])
        edges_i = work[0:2 * CHUNKS, 0:EC].bitcast(I32)
        edges_f = work[0:2 * CHUNKS, SC:SC + EC]
        att_bc = work[:, 2 * SC:2 * SC + 2 * H * C].rearrange("p (a n) -> p a n", a=2)
        att_junk = work[:, 2 * SC + 2 * H * C:2 * SC + 2 * H * C + C]
        ids_i = work[:, 4 * SC:4 * SC + NW * WINDOW // 2].bitcast(I32)
        buf_E = work[:, 0:EC]
        buf_keep = work[:, SC:SC + EC + 1]
        buf_reset = work[:, 2 * SC:2 * SC + EC + 1]
        buf_F = work[:, 3 * SC:3 * SC + EC]
        buf_B = work[:, 4 * SC:4 * SC + EC]
        dst_scan_f = work[:, 3 * SC:3 * SC + EC + 2]
        dst_scan_i = work[:, 4 * SC:4 * SC + EC + 2].bitcast(I32)
        o = 0
        rows = work[0:BLK, o:o + G_RING * D].rearrange("p (s d) -> p s d", s=G_RING)
        o += G_RING * D
        spread = work[0:BLK, o:o + A_RING * P].rearrange("p (s n) -> p s n", s=A_RING)
        o += A_RING * P
        stage = [work[:, o + j * 2 * H * P:o + (j + 1) * 2 * H * P].rearrange("p (m n) -> p m n", n=P)
                 for j in range(2)]
        o += 4 * H * P
        aggt = [work[:, o + j * 2 * H * P:o + (j + 1) * 2 * H * P].rearrange("p (m n) -> p m n", n=P)
                for j in range(2)]
        assert o + 4 * H * P <= 5 * SC

        stats = sb("stats", [P, TILES, 6])
        mean = sb("mean", [P, TILES])
        rstd = sb("rstd", [P, TILES])
        half = sb("half", [P, TILES])
        inv_tmp = sb("inv_tmp", [P, TILES])
        xn = [sb(f"xn{j}", [P, D]) for j in range(UNROLL)]
        xnT = [sb(f"xnT{j}", [P, D]) for j in range(UNROLL)]
        score_all = sb("score_all", [P, TILES, 2 * H])
        idx_stage = [sb(f"idx_stage{j}", [BLK, 2 * CHUNKS], I32) for j in range(UNROLL)]
        got_src = [sb(f"got_src{j}", [BLK, CHUNKS, H]) for j in range(UNROLL)]
        got_dst = [sb(f"got_dst{j}", [BLK, CHUNKS, H]) for j in range(UNROLL)]
        edge_e = [sb(f"edge_e{j}", [BLK, P]) for j in range(UNROLL)]
        cols = sb("cols", [P, 8])
        chain_rows = sb("chain_rows", [1, 4 * P + 4])
        idx_row = [sb(f"idx_row{j}", [BLK, IDX_GROUP], I32) for j in range(G_RING // IDX_GROUP)]

        y1 = [sb(f"y1_{j}", [P, D]) for j in range(2)]
        tn = [sb(f"tn{j}", [P, D]) for j in range(2)]
        res = [sb(f"res{j}", [P, D]) for j in range(2)]
        comb = [sb(f"comb{j}", [P, NX]) for j in range(2)]
        small = [sb(f"small{j}", [P, 80]) for j in range(2)]
        top_idx = [sb(f"top_idx{j}", [P, 8], U32) for j in range(2)]
        tT = [sb(f"tT{j}", [P, 2, P]) for j in range(2)]
        combT = sb("combT", [NX, P])
        h_sb = [sb(f"h_sb{j}", [P, 2, P]) for j in range(2)]

        banks = ctx.enter_context(nc.psum_tensor("banks", [P, 8, 512], F32))
        bank = [banks[:, j, :] for j in range(8)]

        in_x, in_edges, in_att, in_W, in_weights, in_small, in_scan = (
            sem("in_x"), sem("in_edges"), sem("in_att"), sem("in_W"), sem("in_weights"), sem("in_small"), sem("in_scan"))
        in_win = sem("in_win")
        dve_chain, pool_chain, act_chain = sem("dve_chain"), sem("pool_chain"), sem("act_chain")
        dve_mark, pool_mark = sem("dve_mark"), sem("pool_mark")
        consts_ready = sem("consts_ready")
        x_pad, zero_ready = sem("x_pad"), sem("zero_ready")
        edges_ready = sem("edges_ready")
        edgesT_done, idx_ready = sem("edgesT_done"), sem("idx_ready")
        va_ready = sem("va_ready")
        xn_ready, xnT_done, xnT_ready, score_done, score_copied = (
            sem("xn_ready"), sem("xnT_done"), sem("xnT_ready"), sem("score_done"), sem("score_copied"))
        xn_stored = [sem(f"xn_stored{j}") for j in range(UNROLL)]
        tables_stored = sem("tables_stored")
        scan_pad = sem("scan_pad")
        idx_staged = sem("idx_staged")
        got = [sem(f"got{j}") for j in range(UNROLL)]
        edge_ready, edgeT_done, edge_copied = sem("edge_ready"), sem("edgeT_done"), sem("edge_copied")
        col_ready, row_done, row_ready, col_done = sem("col_ready"), sem("row_done"), sem("row_ready"), sem("col_done")
        exp_in, exp_out = sem("exp_in"), sem("exp_out")
        alpha_scan, alphaT_done, alpha_ready = sem("alpha_scan"), sem("alphaT_done"), sem("alpha_ready")
        win_ready = sem("win_ready")
        rows_in = [sem(f"rows_in{j}") for j in range(G_RING)]
        rows_free, spread_ready, spread_free = sem("rows_free"), sem("spread_ready"), sem("spread_free")
        win_done, acc_free = sem("win_done"), sem("acc_free")
        stage_out = [sem(f"stage_out{j}") for j in range(2)]
        bias_added = sem("bias_added")
        agg_in = [sem(f"agg_in{j}") for j in range(2)]
        proj_done, tn_ready, tr_done, tT_ready = sem("proj_done"), sem("tn_ready"), sem("tr_done"), sem("tT_ready")
        logit_done, shift_ready, exp_ready = sem("logit_done"), sem("shift_ready"), sem("exp_ready")
        comb_ready, combT_done, combT_ready, b2_done = (
            sem("comb_ready"), sem("combT_done"), sem("combT_ready"), sem("b2_done"))
        hT_done, h_ready, y_done, y_free = sem("hT_done"), sem("h_ready"), sem("y_done"), sem("y_free")
        out_stored = [sem(f"out_stored{j}") for j in range(2)]

        scan_dst = dst.rearrange("(c j) -> c j", c=CHUNKS)
        block = ctx.enter_context(nc.Block())

        @block.sync
        def _(sp):
            sp.dma_start(edges_i[0:CHUNKS, :], src.rearrange("(c j) -> c j", c=CHUNKS)).then_inc(in_edges, 16)
            sp.dma_start(edges_i[CHUNKS:, :], scan_dst).then_inc(in_edges, 16)
            sp.wait_ge(x_pad, 1)
            sp.dma_start(x_all[:, 0:FULL, :], x[0:FULL * P, :].rearrange("(t p) d -> p t d", p=P)).then_inc(in_x, 16)
            sp.dma_start(x_all[0:LAST, FULL, :], x[FULL * P:N, :]).then_inc(in_x, 16)
            sp.dma_start(W_sb[:, :, :], W.rearrange("(k p) n -> p k n", p=P)).then_inc(in_W, 16)
            for a, att in enumerate((att_src, att_dst)):
                sp.dma_start(att_bc[:, a, :], att.rearrange("h c -> (h c)").partition_broadcast(P)).then_inc(in_att, 16)
            sp.dma_start(win_end[0:1, 1:NB], dst.rearrange("(a b j) -> a b j", a=1, j=BLK)[:, 0:NB - 1, BLK - 1],
                         allow_slow_non_contiguous=True)\
                .then_inc(in_win, 16)
            sp.dma_start(bias_bc[:, :], gnn_bias.partition_broadcast(P)).then_inc(in_small, 16)
            sp.dma_start(b2_sb[:, :], b2).then_inc(in_small, 16)
            for k in range(2):
                sp.dma_start(router_sb[:, k, :], router_w[:, k * P:(k + 1) * P].rearrange("e p -> p e"),
                             allow_slow_non_contiguous=True).then_inc(in_small, 16)
                sp.dma_start(b1_sb[:, :, k], b1[:, k * P:(k + 1) * P].rearrange("e p -> p e"),
                             allow_slow_non_contiguous=True).then_inc(in_small, 16)
            sp.wait_ge(scan_pad, 2)
            for h in range(H):
                r = h * CHUNKS
                sp.dma_start(dst_scan_i[r:r + CHUNKS, 1:EC + 1], scan_dst).then_inc(in_scan, 16)
                sp.dma_start(dst_scan_i[r + 1:r + CHUNKS, 0:1], scan_dst[0:CHUNKS - 1, EC - 1:EC],
                             allow_slow_non_contiguous=True).then_inc(in_scan, 16)
                sp.dma_start(dst_scan_i[r:r + CHUNKS - 1, EC + 1:EC + 2], scan_dst[1:CHUNKS, 0:1],
                             allow_slow_non_contiguous=True).then_inc(in_scan, 16)
            for e in range(NX):
                sp.dma_start(w1_sb[:, e, :, :], w1[e].rearrange("(k p) n -> p k n", p=P)).then_inc(in_weights, 16)
                sp.dma_start(w2_sb[:, e, :, :], w2[e].rearrange("(k p) n -> p k n", p=P)).then_inc(in_weights, 16)
            with sp.Fori(0, TILES // UNROLL) as i:
                for j in range(UNROLL):
                    sp.wait_ge(xn_ready, i * UNROLL + (j + 1))
                    sp.dma_start(xn_table.rearrange("(t p) d -> t p d", p=P)[bass.ds(i * UNROLL + j, 1), :, :]
                                 .rearrange("t p d -> (t p) d"), xn[j][:, :]).then_inc(xn_stored[j], 16)
            sp.wait_ge(score_copied, TILES)
            sp.dma_start(score_src_table.rearrange("(t p) h -> p t h", p=P), score_all[:, :, 0:H]).then_inc(tables_stored, 16)
            sp.dma_start(score_dst_table.rearrange("(t p) h -> p t h", p=P), score_all[:, :, H:]).then_inc(tables_stored, 16)
            def store_stage(j, n):
                sp.wait_ge(acc_free, (n * 2 + (j + 1)) * WIN_PER_TILE + ACC_RING)
                sp.dma_start(agg_table[bass.ds(n * 2 + j, 1), :, :].rearrange("t p n -> (t p) n"),
                             stage[j].rearrange("p m n -> p (m n)")).then_inc(stage_out[j], 16)

            with sp.Fori(0, TILES // 2) as i:
                store_stage(0, i)
                store_stage(1, i)
            store_stage(0, TILES // 2)

            def load_agg(j, n):
                sp.wait_ge(stage_out[j], (n + 1) * 16)
                sp.dma_start(aggt[j].rearrange("p m n -> p (m n)"),
                             agg_table[bass.ds(n * 2 + j, 1), :, :].rearrange("t p n -> (t p) n")).then_inc(agg_in[j], 16)

            def store_out(j, n):
                sp.wait_ge(y_free, (n * 2 + (j + 1)) * NX + 2)
                sp.dma_start(out[bass.ds((n * 2 + j) * P, P), :], res[j][:, :]).then_inc(out_stored[j], 16)

            load_agg(0, 0)
            load_agg(1, 0)
            with sp.Fori(0, TILES // 2 - 1) as i:
                for j in range(2):
                    sp.wait_ge(proj_done, i * 2 + (j + 1))
                    load_agg(j, i + 1)
                for j in range(2):
                    store_out(j, i)
            last = TILES // 2
            sp.wait_ge(proj_done, TILES - 2)
            load_agg(0, last)
            store_out(0, last - 1)
            store_out(1, last - 1)
            sp.wait_ge(y_free, TILES * NX + 2)
            sp.dma_start(out[FULL * P:N, :], res[0][0:LAST, :]).then_inc(out_stored[0], 16)
            sp.wait_ge(out_stored[0], 16 * (last + 1))
            sp.wait_ge(out_stored[1], 16 * last)

        @block.gpsimd
        def _(pool):
            count = [0]

            def link(ins):
                count[0] += 1
                ins.then_inc(pool_chain, 1)
                pool.wait_ge(pool_chain, count[0])

            pool.memset(x_all[:, FULL, :], 0.0).then_inc(x_pad, 1)
            link(pool.memset(ident[:, :], 0.0))
            pool.affine_select(out=ident[:, :], in_=ident[:, :], compare_op=ALU.not_equal, fill=1.0, base=0,
                               pattern=[[-1, P]], channel_multiplier=1).then_inc(consts_ready, 1)
            link(pool.iota(expert_ids_i[:, :], pattern=[[1, NX]], base=0, channel_multiplier=0))
            pool.tensor_copy(expert_ids[:, :], expert_ids_i[:, :]).then_inc(consts_ready, 1)
            HALF_IDS = NW * WINDOW // 2
            for n in range(2):
                link(pool.iota(ids_i[:, 0:HALF_IDS], pattern=[[1, HALF_IDS]], base=n * HALF_IDS, channel_multiplier=0))
                link(pool.tensor_copy(node_ids[:, n * HALF_IDS:(n + 1) * HALF_IDS], ids_i[:, 0:HALF_IDS]))
            pool.memset(dst_scan_i[:, 0:1], -1).then_inc(scan_pad, 1)
            pool.memset(dst_scan_i[:, EC + 1:EC + 2], -1).then_inc(scan_pad, 1)

            pool.wait_ge(idx_ready, 1)
            pool.wait_ge(tables_stored, 32)
            with pool.Fori(0, KB // UNROLL) as i:
                for j in range(UNROLL):
                    pool.wait_ge(edge_ready, i * UNROLL + j)
                    pool.tensor_copy(idx_stage[j][:, :], idx_k[:, bass.ds(i * UNROLL + j, 1), :]).then_inc(idx_staged, 1)
                    pool.wait_ge(idx_staged, i * UNROLL + (j + 1))
                    pool.sem_inc(pool_mark, 1)
                    for c in range(CHUNKS):
                        pool.indirect_dma_start(got_src[j][:, c, :], None, score_src_table,
                                                bass.IndirectOffsetOnAxis(idx_stage[j][:, c:c + 1], 0)).then_inc(got[j], 16)
                        pool.indirect_dma_start(got_dst[j][:, c, :], None, score_dst_table,
                                                bass.IndirectOffsetOnAxis(idx_stage[j][:, CHUNKS + c:CHUNKS + c + 1], 0))\
                            .then_inc(got[j], 16)
            pool.wait_ge(in_small, 16 * 6)
            with pool.Fori(0, TILES) as t:
                pool.tensor_tensor(x_all[:, bass.ds(t, 1), :], x_all[:, bass.ds(t, 1), :], bias_bc[:, :].unsqueeze(1), ALU.add)\
                    .then_inc(bias_added, 1)

            pool.wait_ge(alpha_ready, KB)
            for j in range(UNROLL):
                pool.wait_ge(xn_stored[j], 16 * (TILES // UNROLL))
            with pool.Fori(0, NB // G_RING) as i:
                for q in range(G_RING // IDX_GROUP):
                    pool.wait_ge(rows_free, i * G_RING + (q * IDX_GROUP + IDX_GROUP - 1))
                    pool.tensor_copy(idx_row[q][:, :], src_b[:, bass.ds(i * G_RING + q * IDX_GROUP, IDX_GROUP)])\
                        .then_inc(idx_staged, 1)
                    pool.wait_ge(idx_staged, i * (G_RING // IDX_GROUP) + (KB + q + 1))
                    for k in range(IDX_GROUP):
                        s = q * IDX_GROUP + k
                        pool.wait_ge(rows_free, i * G_RING + (s + 1))
                        pool.sem_inc(pool_mark, 1)
                        pool.indirect_dma_start(rows[:, s, :], None, xn_table,
                                                bass.IndirectOffsetOnAxis(idx_row[q][:, k:k + 1], 0)).then_inc(rows_in[s], 16)

        @block.tensor
        def _(pe):
            pe.wait_ge(consts_ready, 2)
            pe.wait_ge(edges_ready, 1)
            for k in range(KB):
                m = pe.transpose(bank[k // 16][0:BLK, (k % 16) * 32:(k % 16) * 32 + 32],
                                 edges_f[:, k * BLK:(k + 1) * BLK], ident[0:32, 0:32])
            m.then_inc(edgesT_done, 1)
            pe.wait_ge(va_ready, 1)
            with pe.Fori(0, TILES // UNROLL) as i:
                for j in range(UNROLL):
                    pe.wait_ge(xn_ready, i * UNROLL + (j + 1))
                    pe.wait_ge(score_copied, i * UNROLL)
                    pe.transpose(bank[2 + j][:, 0:P], xn[j][:, 0:P], ident[:, :])
                    pe.transpose(bank[2 + j][:, P:D], xn[j][:, P:D], ident[:, :]).then_inc(xnT_done, 1)
                for j in range(UNROLL):
                    pe.wait_ge(xnT_ready, i * UNROLL + (j + 1))
                    for k in range(2):
                        m = pe.matmul(bank[2 + j][:, D:D + 2 * H], xnT[j][:, k * P:(k + 1) * P], va[:, k, :],
                                      start=(k == 0), stop=(k == 1))
                    m.then_inc(score_done, 1)
            with pe.Fori(0, KB // UNROLL) as i:
                for j in range(UNROLL):
                    pe.wait_ge(edge_ready, i * UNROLL + (j + 1))
                    pe.wait_ge(edge_copied, i * UNROLL)
                    pe.transpose(bank[2 + j][:, 0:BLK], edge_e[j][:, :], ident[0:BLK, 0:BLK]).then_inc(edgeT_done, 1)
            for n in range(4):
                pe.wait_ge(col_ready, n + 1)
                pe.transpose(bank[0][0:1, 0:P], cols[:, 0:1], ident[:, :])
                pe.transpose(bank[0][0:1, P:2 * P], cols[:, 1:2], ident[:, :]).then_inc(row_done, 1)
                pe.wait_ge(row_ready, n + 1)
                pe.transpose(bank[1][:, 0:1], chain_rows[0:1, 3 * P + 1 + n % 2:4 * P + 1 + n % 2],
                             ident[0:1, 0:1]).then_inc(col_done, 1)
            pe.wait_ge(alpha_scan, 1)
            for k in range(KB):
                if k >= UNROLL:
                    pe.wait_ge(alpha_ready, k - UNROLL + 1)
                pe.transpose(bank[2 + k % UNROLL][0:BLK, 0:P], buf_E[:, k * BLK:(k + 1) * BLK], ident[:, :])\
                    .then_inc(alphaT_done, 1)

            pe.wait_ge(alpha_ready, KB)
            pe.wait_ge(win_ready, 1)
            pe.sem_inc(rows_free, G_RING - 1)
            pe.sem_inc(spread_free, A_RING)

            def step(b_slot, w, s, first):
                pe.wait_ge(spread_ready, s + 1)
                for k in range(2):
                    m = pe.matmul(banks[:, bass.ds(w % ACC_RING, 1), k * P:(k + 1) * P], rows[:, b_slot, k * P:(k + 1) * P],
                                  spread[:, bass.ds(s % A_RING, 1), :], start=(first and k == 0), stop=True,
                                  skip_group_check=True)
                    if k == 0:
                        m.then_inc(win_done if first else rows_free, 1)
                m.then_inc(spread_free, 1)

            pe.wait_ge(zero_ready, 1)
            pe.matmul(bank[0][:, 0:D], zeros[:, 0:P], zeros[:, :], start=True, stop=True, skip_group_check=True)
            with pe.Fori(0, NB // G_RING) as i:
                b0 = i * G_RING
                w = pe.value_load(win_end[0:1, bass.ds(b0, 1)], min_val=0, max_val=NW - 1)
                for k in range(G_RING):
                    pe.wait_ge(rows_in[k], i * 16 + 16)
                    step(k, w, b0 + k + w, False)
                    w_end = pe.value_load(win_end[0:1, bass.ds(b0 + (k + 1), 1)], min_val=0, max_val=NW - 1)
                    with pe.If(w_end > w):
                        with pe.Fori(w + 1, w_end + 1) as v:
                            pe.wait_ge(acc_free, v + 1)
                            step(k, v, b0 + k + v, True)
                    w = w_end
            pe.drain().then_inc(win_done, 1)

            pe.wait_ge(in_weights, 16 * 2 * NX)
            pe.wait_ge(acc_free, NW + ACC_RING)

            def project(j, n):
                pe.wait_ge(agg_in[j], (n + 1) * 16)
                for k in range(2):
                    for h in range(H):
                        m = pe.matmul(bank[0][:, 0:C], aggt[j][:, k * H + h, :], W_sb[:, k, h * C:(h + 1) * C],
                                      start=(k == 0 and h == 0), stop=(k == 1 and h == H - 1))
                m.then_inc(proj_done, 1)

            def router(j, t):
                pe.wait_ge(tn_ready, t + 1)
                for k in range(2):
                    m = pe.transpose(bank[1][:, k * P:(k + 1) * P], tn[j][:, k * P:(k + 1) * P], ident[:, :])
                m.then_inc(tr_done, 1)
                pe.wait_ge(tT_ready, t + 1)
                for k in range(2):
                    m = pe.matmul(bank[1][:, D:D + NX], tT[j][:, k, :], router_sb[:, k, :], start=(k == 0), stop=(k == 1))
                m.then_inc(logit_done, 1)

            def bias_mix(j, t):
                pe.wait_ge(comb_ready, t + 1)
                pe.transpose(bank[1][0:NX, 384:384 + P], comb[j][:, :], ident[:, :]).then_inc(combT_done, 1)
                pe.wait_ge(combT_ready, t + 1)
                pe.matmul(bank[5][:, 0:D], combT[:, :], b2_sb[:, :], start=True, stop=True).then_inc(b2_done, 1)

            def up(j, e):
                for f in range(2):
                    for k in range(2):
                        m = pe.matmul(bank[2 + e % 2][:, f * P:(f + 1) * P], w1_sb[:, e, k, f * P:(f + 1) * P],
                                      tT[j][:, k, :], start=(k == 0), stop=(k == 1))
                m.then_inc(hT_done, 1)

            def down(j, e, t):
                pe.wait_ge(h_ready, t * NX + (e + 1))
                pe.wait_ge(y_free, t * NX + (e + 1))
                for f in range(2):
                    m = pe.matmul(bank[6 + e % 2][:, 0:D], h_sb[e % 2][:, f, :], w2_sb[:, e, f, :],
                                  start=(f == 0), stop=(f == 1))
                m.then_inc(y_done, 1)

            def tile(j, n, ahead):
                t = n * 2 + j
                up(j, 0)
                if ahead:
                    project(1 - j, n + j)
                for e in range(NX):
                    if e + 1 < NX:
                        up(j, e + 1)
                    down(j, e, t)
                    if ahead and e == 3:
                        router(1 - j, t + 1)
                if ahead:
                    bias_mix(1 - j, t + 1)

            project(0, 0)
            router(0, 0)
            bias_mix(0, 0)
            with pe.Fori(0, TILES // 2) as i:
                tile(0, i, True)
                tile(1, i, True)
            tile(0, TILES // 2, False)

        @block.scalar
        def _(act):
            with act.Fori(0, TILES // UNROLL) as i:
                for j in range(UNROLL):
                    act.wait_ge(xnT_done, i * UNROLL + (j + 1))
                    act.copy(xnT[j][:, :], bank[2 + j][:, 0:D]).then_inc(xnT_ready, 1)
                for j in range(UNROLL):
                    act.wait_ge(score_done, i * UNROLL + (j + 1))
                    act.copy(score_all[:, bass.ds(i * UNROLL + j, 1), :], bank[2 + j][:, D:D + 2 * H].unsqueeze(1))\
                        .then_inc(score_copied, 1)
            with act.Fori(0, KB // UNROLL) as i:
                for j in range(UNROLL):
                    act.wait_ge(edgeT_done, i * UNROLL + (j + 1))
                    act.copy(buf_E[:, bass.ds((i * UNROLL + j) * BLK, BLK)], bank[2 + j][:, 0:BLK]).then_inc(edge_copied, 1)
            act.wait_ge(exp_in, 1)
            act.activation(buf_E[:, :], buf_E[:, :], ACT.Exp).then_inc(exp_out, 1)
            alpha_v = alpha[:, :, :].rearrange("p (c k) h -> p k h c", k=KB)
            for k in range(KB):
                act.wait_ge(alphaT_done, k + 1)
                act.copy(alpha_v[:, k, :, :], bank[2 + k % UNROLL][0:BLK, 0:P].rearrange("p (h c) -> p h c", h=H))\
                    .then_inc(alpha_ready, 1)
            act.sem_inc(acc_free, ACC_RING)

            def tile_out(j, n):
                act.wait_ge(stage_out[j], n * 16)
                for v in range(WIN_PER_TILE):
                    act.wait_ge(win_done, (n * 2 + j) * WIN_PER_TILE + (v + 1))
                    act.copy(stage[j][:, :, v * WINDOW:(v + 1) * WINDOW],
                                 bank[v % ACC_RING][:, 0:2 * H * WINDOW].rearrange("p (m n) -> p m n", n=WINDOW)).then_inc(acc_free, 1)

            with act.Fori(0, TILES // 2) as i:
                tile_out(0, i)
                tile_out(1, i)
            tile_out(0, TILES // 2)

            act.wait_ge(in_small, 16 * 6)

            def route(j, t):
                act.wait_ge(tr_done, t + 1)
                act.copy(tT[j][:, :, :], bank[1][:, 0:D].rearrange("p (k n) -> p k n", k=2)).then_inc(tT_ready, 1)
                act.wait_ge(shift_ready, t + 1)
                act.activation(small[j][:, 8:8 + NX], bank[1][:, D:D + NX], ACT.Exp, bias=small[j][:, 0:1],
                               accum_out=small[j][:, 1:2]).then_inc(exp_ready, 1)

            def mix(t):
                act.wait_ge(combT_done, t + 1)
                act.copy(combT[:, :], bank[1][0:NX, 384:384 + P]).then_inc(combT_ready, 1)

            def gelus(e, t):
                act.wait_ge(hT_done, t * NX + (e + 1))
                for f in range(2):
                    g = act.activation(h_sb[e % 2][:, f, :], bank[2 + e % 2][:, f * P:(f + 1) * P], ACT.Gelu,
                                       bias=b1_sb[:, e, f:f + 1])
                g.then_inc(h_ready, 1)

            def tile(j, n, ahead):
                t = n * 2 + j
                for e in range(NX):
                    gelus(e, t)
                    if ahead and e == 4:
                        route(1 - j, t + 1)
                if ahead:
                    mix(t + 1)

            route(0, 0)
            mix(0)
            with act.Fori(0, TILES // 2) as i:
                tile(0, i, True)
                tile(1, i, True)
            tile(0, TILES // 2, False)

        @block.vector
        def _(dve):
            count = [0]

            def link(ins):
                count[0] += 1
                ins.then_inc(dve_chain, 1)
                dve.wait_ge(dve_chain, count[0])

            dve.memset(zeros[:, :], 0.0).then_inc(zero_ready, 1)
            def inv_sqrt(chained, y, var, t, half_v):
                chained(dve.tensor_scalar(half_v, var, LN_EPS, None, ALU.add))
                chained(dve.tensor_single_scalar(t.bitcast(I32), half_v.bitcast(I32), 1, op=ALU.arith_shift_right))
                chained(dve.tensor_scalar(y.bitcast(I32), t.bitcast(I32), -1.0, RSQRT_MAGIC, ALU.mult, ALU.add))
                chained(dve.tensor_scalar(half_v, half_v, -0.5, None, ALU.mult))
                for _ in range(NEWTON_STEPS):
                    chained(dve.tensor_tensor(t, y, y, ALU.mult))
                    chained(dve.tensor_tensor(t, t, half_v, ALU.mult))
                    chained(dve.scalar_tensor_tensor(y, t, 1.5, y, ALU.add, ALU.mult))

            link(dve.memset(win_end[0:1, NB:NB + 1], NW - 1))
            link(dve.memset(win_end[0:1, 0:1], 0))
            dve.wait_ge(in_edges, 32)
            dve.tensor_copy(edges_f, edges_i).then_inc(edges_ready, 1)
            dve.wait_ge(in_x, 32)
            with dve.Fori(0, TILES) as t:
                dve.bn_stats(stats[:, bass.ds(t, 1), :].rearrange("p t s -> p (t s)"),
                             x_all[:, bass.ds(t, 1), :].rearrange("p t d -> p (t d)")).then_inc(dve_chain, 1)
            count[0] += TILES
            dve.wait_ge(dve_chain, count[0])
            link(dve.tensor_tensor(mean[:, :], stats[:, :, 1], stats[:, :, 4], ALU.add))
            link(dve.tensor_scalar(mean[:, :], mean[:, :], 0.5, None, ALU.mult))
            link(dve.tensor_tensor(half[:, :], stats[:, :, 1], stats[:, :, 4], ALU.subtract))
            link(dve.tensor_scalar(half[:, :], half[:, :], 0.5, None, ALU.mult))
            link(dve.tensor_tensor(half[:, :], half[:, :], half[:, :], ALU.mult))
            link(dve.tensor_tensor(rstd[:, :], stats[:, :, 2], stats[:, :, 5], ALU.add))
            link(dve.scalar_tensor_tensor(rstd[:, :], rstd[:, :], 1.0 / D, half[:, :], ALU.mult, ALU.add))
            inv_sqrt(link, rstd[:, :], rstd[:, :], half[:, :], inv_tmp[:, :])
            dve.wait_ge(in_att, 32)
            dve.wait_ge(in_W, 16)
            for a in range(2):
                for k in range(2):
                    for h in range(H):
                        link(dve.tensor_tensor_reduce(out=att_junk, in0=W_sb[:, k, h * C:(h + 1) * C],
                                                      in1=att_bc[:, a, h * C:(h + 1) * C], scale=1.0, scalar=0.0,
                                                      op0=ALU.mult, op1=ALU.add,
                                                      accum_out=va[:, k, a * H + h:a * H + h + 1]))
            dve.sem_inc(va_ready, 1)
            with dve.Fori(0, TILES // UNROLL) as i:
                for j in range(UNROLL):
                    dve.wait_ge(xn_stored[j], i * 16)
                    dve.wait_ge(xnT_done, i * UNROLL)
                    dve.tensor_scalar(xn[j][:, :].unsqueeze(1), x_all[:, bass.ds(i * UNROLL + j, 1), :],
                                      mean[:, bass.ds(i * UNROLL + j, 1)], rstd[:, bass.ds(i * UNROLL + j, 1)],
                                      ALU.subtract, ALU.mult).then_inc(xn_ready, 1)
            dve.wait_ge(edgesT_done, 1)
            for n, (k0, k1) in enumerate(((0, 16), (16, KB))):
                v = bank[n][0:BLK, 0:(k1 - k0) * 32].rearrange("p (k c) -> p k c", c=32)
                link(dve.tensor_copy(src_b[:, :].rearrange("p (c k) -> p k c", k=KB)[:, k0:k1, :], v[:, :, 0:CHUNKS]))
                link(dve.tensor_copy(dst_f[:, :].rearrange("p (c k) -> p k c", k=KB)[:, k0:k1, :], v[:, :, CHUNKS:]))
                link(dve.tensor_copy(idx_k[:, k0:k1, :], v))
            dve.sem_inc(idx_ready, 1)
            dve.wait_ge(in_win, 16)
            dve.tensor_single_scalar(win_end[0:1, 1:NB], win_end[0:1, 1:NB], 4, op=ALU.arith_shift_right)\
                .then_inc(win_ready, 1)
            dve.wait_ge(in_scan, 16 * 3 * H)
            link(dve.tensor_copy(dst_scan_f, dst_scan_i))
            link(dve.tensor_tensor(buf_keep, dst_scan_f[:, 0:EC + 1], dst_scan_f[:, 1:EC + 2], ALU.is_equal))
            link(dve.tensor_scalar(buf_reset, buf_keep, 1.0, BIG, ALU.subtract, ALU.mult))
            link(dve.tensor_reduce(cols[:, 2:3], buf_keep[:, 0:EC], AX_X, ALU.min))
            link(dve.tensor_reduce(cols[:, 3:4], buf_keep[:, 1:EC + 1], AX_X, ALU.min))
            link(dve.tensor_scalar(cols[:, 4:6], cols[:, 2:4], 1.0, BIG, ALU.subtract, ALU.mult))
            base = count[0]
            with dve.Fori(0, KB // UNROLL) as i:
                for j in range(UNROLL):
                    dve.wait_ge(got[j], i * (16 * 2 * CHUNKS) + 16 * 2 * CHUNKS)
                    dve.wait_ge(edgeT_done, i * UNROLL)
                    dve.tensor_tensor(got_src[j][:, :, :], got_src[j][:, :, :], got_dst[j][:, :, :], ALU.add)\
                        .then_inc(dve_chain, 1)
                    dve.wait_ge(dve_chain, i * UNROLL + (base + j + 1))
                    dve.scalar_tensor_tensor(edge_e[j][:, :].rearrange("p (h c) -> p c h", h=H), got_src[j][:, :, :], NEG_SLOPE,
                                             got_src[j][:, :, :], ALU.mult, ALU.max).then_inc(edge_ready, 1)
            count[0] += KB
            dve.wait_ge(edge_copied, KB)

            turn = [0]

            def chained_scan(res_v, data0, data1, all_keep, op0, op1, init, back):
                n = turn[0]
                turn[0] += 1
                r = (lambda a: a[:, ::-1]) if back else (lambda a: a)
                end = res_v[:, 0:1] if back else res_v[:, EC - 1:EC]
                link(dve.tensor_tensor_scan(r(res_v), r(data0), r(data1), init, op0, op1))
                link(dve.tensor_copy(cols[:, 1:2], all_keep))
                dve.tensor_copy(cols[:, 0:1], end).then_inc(col_ready, 1)
                dve.wait_ge(row_done, n + 1)
                link(dve.tensor_copy(chain_rows[0:1, 0:2 * P], bank[0][0:1, 0:2 * P]))
                vals, keeps = chain_rows[0:1, 0:P], chain_rows[0:1, P:2 * P]
                shifted = chain_rows[0:1, 3 * P + 1 + n % 2:4 * P + 1 + n % 2]
                link(dve.memset(chain_rows[0:1, 3 * P:4 * P + 4], init))
                outs = chain_rows[0:1, 2 * P:3 * P]
                link(dve.tensor_tensor_scan(r(outs), r(keeps), r(vals), init, op0, op1))
                if back:
                    dve.tensor_copy(shifted[:, 0:P - 1], outs[:, 1:P]).then_inc(row_ready, 1)
                else:
                    dve.tensor_copy(shifted[:, 1:P], outs[:, 0:P - 1]).then_inc(row_ready, 1)
                dve.wait_ge(col_done, n + 1)
                link(dve.tensor_copy(cols[:, 6:7], bank[1][:, 0:1]))
                link(dve.tensor_tensor_scan(r(res_v), r(data0), r(data1), cols[:, 6:7], op0, op1))

            chained_scan(buf_F, buf_reset[:, 0:EC], buf_E, cols[:, 4:5], ALU.add, ALU.max, -BIG, False)
            chained_scan(buf_B, buf_reset[:, 1:EC + 1], buf_E, cols[:, 5:6], ALU.add, ALU.max, -BIG, True)
            link(dve.tensor_tensor(buf_F, buf_F, buf_B, ALU.max))
            dve.tensor_tensor(buf_E, buf_E, buf_F, ALU.subtract).then_inc(exp_in, 1)
            dve.wait_ge(exp_out, 1)
            chained_scan(buf_F, buf_keep[:, 0:EC], buf_E, cols[:, 2:3], ALU.mult, ALU.add, 0.0, False)
            chained_scan(buf_B, buf_keep[:, 1:EC + 1], buf_E, cols[:, 3:4], ALU.mult, ALU.add, 0.0, True)
            link(dve.tensor_tensor(buf_B, buf_B, buf_E, ALU.subtract))
            link(dve.scalar_tensor_tensor(buf_F, buf_F, SOFTMAX_EPS, buf_B, ALU.add, ALU.add))
            link(dve.reciprocal(buf_F, buf_F))
            dve.tensor_tensor(buf_E, buf_E, buf_F, ALU.mult).then_inc(alpha_scan, 1)

            dve.wait_ge(alpha_ready, KB)

            def spread_step(b, w, s):
                dve.wait_ge(spread_free, s + 1)
                dve.scalar_tensor_tensor(
                    spread[:, bass.ds(s % A_RING, 1), :].rearrange("p o (h d) -> p (o h) d", h=H),
                    node_ids[0:BLK, bass.ds(w * WINDOW, WINDOW)].unsqueeze(1).to_broadcast([BLK, H, WINDOW]),
                    dst_f[:, bass.ds(b, 1)],
                    alpha[:, bass.ds(b, 1), :].rearrange("p o h -> p (o h)").unsqueeze(2).to_broadcast([BLK, H, WINDOW]),
                    ALU.is_equal, ALU.mult).then_inc(spread_ready, 1)

            with dve.Fori(0, NB // G_RING) as i:
                b0 = i * G_RING
                w = dve.value_load(win_end[0:1, bass.ds(b0, 1)], min_val=0, max_val=NW - 1)
                for k in range(G_RING):
                    spread_step(b0 + k, w, b0 + k + w)
                    w_end = dve.value_load(win_end[0:1, bass.ds(b0 + (k + 1), 1)], min_val=0, max_val=NW - 1)
                    with dve.If(w_end > w):
                        with dve.Fori(w + 1, w_end + 1) as v:
                            spread_step(b0 + k, v, b0 + k + v)
                    w = w_end

            dve.sem_inc(y_free, 2)
            dve.wait_ge(bias_added, TILES)
            head_links, route_links, begin_links = 3 + INV_SQRT_LINKS, 11, 2
            per_tile = head_links + route_links + begin_links
            start = count[0]

            def linker(t, at):
                k = [at]

                def link_t(ins, nop_after=False):
                    k[0] += 1
                    ins.then_inc(dve_chain, 1)
                    dve.wait_ge(dve_chain, t * per_tile + (start + k[0]))
                    if nop_after:
                        dve.sem_inc(dve_mark, 1)
                link_t.count = k
                return link_t

            def normalise(j, t):
                l = linker(t, 0)
                s = small[j]
                dve.wait_ge(proj_done, t + 1)
                l(dve.scalar_tensor_tensor(y1[j][:, :].unsqueeze(1), bank[0][:, 0:D].unsqueeze(1), 1.0 / H,
                                           x_all[:, bass.ds(t, 1), :], ALU.mult, ALU.add))
                l(dve.bn_stats(s[:, 40:46], y1[j][:, :]), True)
                l(dve.bn_aggr(s[:, 46:48], s[:, 40:46]))
                inv_sqrt(l, s[:, 48:49], s[:, 47:48], s[:, 66:67], s[:, 67:68])
                dve.tensor_scalar(tn[j][:, :], y1[j][:, :], s[:, 46:47], s[:, 48:49], ALU.subtract, ALU.mult)\
                    .then_inc(tn_ready, 1)
                assert l.count[0] == head_links

            def route(j, t):
                l = linker(t, head_links)
                s = small[j]
                ex, probs, top, ids = s[:, 8:16], s[:, 16:24], s[:, 24:32], s[:, 32:34]
                dve.wait_ge(logit_done, t + 1)
                dve.tensor_reduce(s[:, 0:1], bank[1][:, D:D + NX], AX_X, ALU.max, negate=True).then_inc(shift_ready, 1)
                dve.wait_ge(exp_ready, t + 1)
                l(dve.reciprocal(s[:, 2:3], s[:, 1:2]))
                l(dve.tensor_scalar(probs, ex, s[:, 2:3], None, ALU.mult), True)
                l(dve.max(top, probs), True)
                l(dve.max_index(top_idx[j][:, :], top, probs))
                l(dve.tensor_copy(ids, top_idx[j][:, 0:2]))
                l(dve.tensor_tensor(s[:, 3:4], top[:, 0:1], top[:, 1:2], ALU.add))
                l(dve.tensor_scalar(s[:, 3:4], s[:, 3:4], 1e-12, None, ALU.max))
                l(dve.reciprocal(s[:, 4:5], s[:, 3:4]))
                l(dve.tensor_scalar(s[:, 50:58], expert_ids[:, :], ids[:, 0:1], s[:, 4:5], ALU.is_equal, ALU.mult))
                l(dve.tensor_scalar(s[:, 58:66], expert_ids[:, :], ids[:, 1:2], s[:, 4:5], ALU.is_equal, ALU.mult))
                l(dve.tensor_tensor(s[:, 50:58], s[:, 50:58], s[:, 58:66], ALU.add))
                dve.tensor_tensor(comb[j][:, :], s[:, 50:58], probs, ALU.mult).then_inc(comb_ready, 1)
                assert l.count[0] == head_links + route_links

            def begin(j, t, n):
                l = linker(t, head_links + route_links)
                dve.wait_ge(out_stored[j], n * 16)
                l(dve.tensor_tensor(res[j][:, :], y1[j][:, :], tn[j][:, :], ALU.add))
                dve.wait_ge(b2_done, t + 1)
                l(dve.tensor_tensor(res[j][:, :], res[j][:, :], bank[5][:, 0:D], ALU.add))

            def mix(j, t, e):
                dve.wait_ge(y_done, t * NX + (e + 1))
                dve.scalar_tensor_tensor(res[j][:, :], bank[6 + e % 2][:, 0:D], comb[j][:, e:e + 1], res[j][:, :],
                                         ALU.mult, ALU.add).then_inc(y_free, 1)
                if e < NX - 1:
                    dve.wait_ge(y_free, t * NX + (e + 3))

            def tile(j, n, ahead):
                t = n * 2 + j
                if ahead:
                    normalise(1 - j, t + 1)
                for e in range(NX):
                    mix(j, t, e)
                    if ahead and e == 3:
                        route(1 - j, t + 1)
                if ahead:
                    begin(1 - j, t + 1, n + j)

            normalise(0, 0)
            route(0, 0)
            begin(0, 0, 0)
            with dve.Fori(0, TILES // 2) as i:
                tile(0, i, True)
                tile(1, i, True)
            tile(0, TILES // 2, False)


_INS = ['x', 'src', 'dst', 'L0_gnn_W', 'L0_gnn_att_src', 'L0_gnn_att_dst', 'L0_gnn_bias', 'L0_ffn_router_w',
        'L0_ffn_w1', 'L0_ffn_b1', 'L0_ffn_w2', 'L0_ffn_b2']


def kernel(**inputs):
    import numpy as _np
    import concourse.bacc as _bacc
    from concourse import mybir as _mybir
    from concourse.bass_utils import run_bass_kernel_spmd as _run

    nc = _bacc.Bacc("TRN2", target_bir_lowering=False, num_devices=1)
    arrays, args = {}, []
    for name in _INS:
        a = _np.ascontiguousarray(inputs[name])
        arrays[f"in_{name}"] = a
        args.append(nc.dram_tensor(f"in_{name}", a.shape, _mybir.dt.from_np(a.dtype), kind="ExternalInput").ap())
    args.append(nc.dram_tensor("out_0", inputs['x'].shape, _mybir.dt.float32, kind="ExternalOutput").ap())
    gat_moe_kernel(nc, *args)
    r = _run(nc, [arrays], core_ids=[0])
    return r.results[0]["out_0"]
```

```python
from contextlib import ExitStack

import concourse.bass as bass
from concourse import mybir

F32 = mybir.dt.float32
I32 = mybir.dt.int32
U32 = mybir.dt.uint32
U8 = mybir.dt.uint8
ALU = mybir.AluOpType
ACT = mybir.ActivationFunctionType
AX_X = mybir.AxisListType.X

P = 128
BIG = 1e30
LN_EPS = 1e-5
SOFTMAX_EPS = 1e-16
NEG_SLOPE = 0.2
RSQRT_MAGIC = float(0x5F3759DF)
NEWTON_STEPS = 3
STAGE2_LINKS = 6
INV_SQRT_LINKS = 4 + 3 * NEWTON_STEPS
CHUNKS = 16
HOME = 32
UNIT = 4
SPREAD = 24
OVER = SPREAD - UNIT
SLOTS = HOME + OVER
HOMES = P // HOME
G_RING = 16
HALF = 8
A_RING = 8
GROUP = 4
ACC_RING = 4
UNROLL = 5


def gat_moe_kernel(nc, x, src, dst, W, att_src, att_dst, gnn_bias, router_w, w1, b1, w2, b2, out):
    N, D = x.shape
    E = src.shape[0]
    H, C = att_src.shape
    NX = router_w.shape[0]
    TILES = -(-N // P)
    FULL = N // P
    LAST = N - FULL * P
    EC = E // CHUNKS
    BLK = P - 3
    KB = EC // BLK
    NB = E // BLK
    NS = TILES * HOMES
    assert EC * CHUNKS == E and KB * BLK == EC and H * CHUNKS == P and D == 2 * P
    assert D == 2 * P and C == D and NB % G_RING == 0 and TILES % UNROLL == 0 and KB % UNROLL == 0
    assert TILES % 2 == 1 and HOMES == ACC_RING and NS <= P and SLOTS * H <= 512 and HOME == 32

    BANK = 512 // (UNIT * H)
    MAX_PLACE = (ACC_RING - 1) * 2 * BANK + HOME // UNIT - 1
    assert MAX_PLACE < 128 and UNIT == 4 and BANK == 16
    ROW = D + H
    node_table = nc.dram_tensor("node_table", [TILES * P, ROW], F32).ap()
    edge_rows = nc.dram_tensor("edge_rows", [CHUNKS, KB, P, D], F32).ap()
    agg_table = nc.dram_tensor("agg_table", [TILES, P, 2 * H * P], F32).ap()

    with ExitStack() as ctx:
        def sb(name, shape, dt=F32):
            return ctx.enter_context(nc.sbuf_tensor(name, shape, dt))

        def sem(name):
            return ctx.enter_context(nc.semaphore(name))

        x_all = sb("x_all", [P, TILES, D])
        W_sb = sb("W_sb", [P, 2, H * C])
        expert_w = sb("expert_w", [P, 2, NX * 2 * D])
        w1_sb = expert_w[:, 0, :].rearrange("p (e k n) -> p e k n", e=NX, k=2)
        w2_sb = expert_w[:, 1, :].rearrange("p (e k n) -> p e k n", e=NX, k=2)
        lo_hot = expert_w[0:BLK, 0, 0:HALF * P].rearrange("p (c n) -> p c n", n=P)
        lo_hotT = [expert_w[:, 0, (1 + j) * HALF * P:(1 + j) * HALF * P + HALF * BLK] for j in range(2)]
        hi_picked = expert_w[0:BLK, 1, 0:HALF * TILES * H].rearrange("p (c n) -> p c n", c=HALF)
        hi_hot = expert_w[0:BLK, 1, 2048:2048 + HALF * TILES].rearrange("p (c n) -> p c n", c=HALF)
        reach_junk = expert_w[:, 1, 2560:2560 + NB]
        first_home_bc = expert_w[:, 1, 3072:3072 + NB]
        last_home_bc = expert_w[:, 1, 3584:3584 + NB]
        alpha = sb("alpha", [BLK, NB, H])
        dst_f = sb("dst_f", [BLK, NB])
        dst_rel = sb("dst_rel", [BLK, NB])
        src_k = sb("src_k", [P, KB, CHUNKS], I32)
        dst_k = sb("dst_k", [BLK, KB + 1, CHUNKS], I32)
        dst_lo = sb("dst_lo", [BLK, KB + 1, CHUNKS])
        dst_hi = sb("dst_hi", [BLK, KB + 1, CHUNKS])
        dst_far = dst_f
        node_ids = sb("node_ids", [P, TILES * P])
        ident = sb("ident", [P, P])
        first_i = sb("first_i", [1, NB], I32)
        last_i = sb("last_i", [1, NB], I32)
        place = sb("place", [1, NB], I32)
        places = sb("places", [1, NB], U8)
        home = sb("home", [1, NB], I32)
        home_f = sb("home_f", [1, NB])
        extras = sb("extras", [1, NB], I32)
        extra_before = sb("extra_before", [1, NB + 1], I32)
        span_f = sb("span_f", [1, NB // GROUP])
        far_f = sb("far_f", [1, 2, NB // G_RING])
        far = sb("far", [1, NB // G_RING], I32)
        step_cols = sb("step_cols", [P, 4])
        steps_to = sb("steps_to", [1, P], I32)
        ones_row = sb("ones_row", [1, P])
        bias_bc = sb("bias_bc", [P, D])
        router_sb = sb("router_sb", [P, 2, NX])
        b1_sb = sb("b1_sb", [P, NX, 2])
        b2_sb = sb("b2_sb", [NX, D])
        va = sb("va", [P, 2, 2 * H])
        expert_ids = sb("expert_ids", [P, NX])
        home_ids = sb("home_ids", [P, 1])
        home_ids_i = sb("home_ids_i", [P, 1], I32)
        expert_ids_i = sb("expert_ids_i", [P, NX], I32)

        zeros = sb("zeros", [P, 1])
        chain_rows = sb("chain_rows", [1, 4 * P + 4])

        SC = EC + 2
        work = sb("work", [P, 5 * SC])
        edges_i = work[0:2 * CHUNKS, 0:EC].bitcast(I32)
        edges_f = work[0:2 * CHUNKS, SC:SC + EC]
        att_bc = work[:, 2 * SC:2 * SC + 2 * H * C].rearrange("p (a n) -> p a n", a=2)
        att_junk = work[:, 2 * SC + 2 * H * C:2 * SC + 2 * H * C + C]
        ids_i = work[:, 4 * SC:4 * SC + TILES * P // 2].bitcast(I32)
        o = 2 * SC + 2 * H * C + C
        row_tmp = work[0:1, o:o + NB].bitcast(I32)
        first_f = work[0:1, o + NB:o + 2 * NB]
        last_home_f = work[0:1, o + 2 * NB:o + 3 * NB]
        extra_sum = work[0:1, o + 3 * NB:o + 4 * NB + 1]
        assert o + 4 * NB + 1 <= 4 * SC
        extra_f = chain_rows[0:1, 0:NB]
        buf_E = work[:, 0:EC]
        buf_keep = work[:, SC:SC + EC + 1]
        buf_reset = work[:, 2 * SC:2 * SC + EC + 1]
        buf_F = work[:, 3 * SC:3 * SC + EC]
        buf_B = work[:, 4 * SC:4 * SC + EC]
        dst_scan_f = work[:, 3 * SC:3 * SC + EC + 2]
        dst_scan_i = work[:, 4 * SC:4 * SC + EC + 2].bitcast(I32)
        got_rows = [work[:, 3 * SC + j * HALF * ROW:3 * SC + (j + 1) * HALF * ROW].rearrange("p (s d) -> p s d", s=HALF)
                    for j in range(2)]
        o = 0
        spread = work[0:BLK, o:o + A_RING * SPREAD * H].rearrange("p (s n) -> p s n", s=A_RING)
        o += A_RING * SPREAD * H
        extra = work[0:BLK, o:o + 2 * HOME * H].rearrange("p (s n) -> p s n", s=2)
        o += 2 * HOME * H
        h_sb = [work[:, o + j * D:o + (j + 1) * D].rearrange("p (k n) -> p k n", k=2) for j in range(3)]
        assert o + 3 * D <= SC
        o = SC
        rows = work[:, o:o + G_RING * D].rearrange("p (s d) -> p s d", s=G_RING)
        o += G_RING * D
        assert o <= 3 * SC
        o = 3 * SC
        stage = [work[:, o + j * 2 * H * P:o + (j + 1) * 2 * H * P].rearrange("p (m n) -> p m n", n=P)
                 for j in range(2)]
        o += 4 * H * P
        aggt = [work[:, a:a + 2 * H * P].rearrange("p (m n) -> p m n", n=P) for a in (SC + G_RING * D, o)]
        assert SC + G_RING * D + 2 * H * P <= 3 * SC and o + 2 * H * P <= 5 * SC

        stats = sb("stats", [P, TILES, 6])
        mean = sb("mean", [P, TILES])
        rstd = sb("rstd", [P, TILES])
        half = sb("half", [P, TILES])
        inv_tmp = sb("inv_tmp", [P, TILES])
        ring1 = sb("ring1", [P, 2 * UNROLL * D])
        xn = [ring1[:, j * D:(j + 1) * D] for j in range(UNROLL)]
        xnT = [ring1[:, (UNROLL + j) * D:(UNROLL + j + 1) * D] for j in range(UNROLL)]
        carry = ring1[:, 0:4 * HOME * H].rearrange("p (s k d h) -> p s k d h", s=2, k=2, h=H)
        o1 = 4 * HOME * H
        hot = ring1[0:BLK, o1:o1 + A_RING * SPREAD].rearrange("p (s d) -> p s d", s=A_RING)
        o1 += A_RING * SPREAD
        extra_hot = ring1[0:BLK, o1:o1 + HOME].unsqueeze(1)
        o1 += HOME
        tT = [ring1[:, o1 + j * D:o1 + (j + 1) * D].rearrange("p (k n) -> p k n", k=2) for j in range(2)]
        assert o1 + 2 * D + P <= 2 * UNROLL * D
        score_all = sb("score_all", [P, TILES, 2 * H])
        idx_stage = [sb(f"idx_stage{j}", [P, HALF], I32) for j in range(2)]
        edge_e = sb("edge_e", [BLK, P])
        edge_z = sb("edge_z", [BLK, HALF, H])
        score_d = [sb(f"score_d{j}", [BLK, HALF, H]) for j in range(2)]
        cols = sb("cols", [P, 8])

        y1 = [sb(f"y1_{j}", [P, D]) for j in range(2)]
        tn = [sb(f"tn{j}", [P, D]) for j in range(2)]
        res = [sb(f"res{j}", [P, D]) for j in range(2)]
        comb = [sb(f"comb{j}", [P, NX]) for j in range(2)]
        small = [sb(f"small{j}", [P, 80]) for j in range(2)]
        top_idx = [sb(f"top_idx{j}", [P, 8], U32) for j in range(2)]
        combT = ring1[0:NX, 2 * UNROLL * D - P:]

        banks = ctx.enter_context(nc.psum_tensor("banks", [P, 8, 512], F32))
        bank = [banks[:, j, :] for j in range(8)]
        h_bank = [bank[2], bank[3], bank[5]]
        y_bank = [bank[6], bank[7], bank[4]]
        sums = banks[:, :, :].rearrange("p (r k) (d h) -> p r k d h", k=2, h=H)
        units = banks[:, :, :].rearrange("p b (q n) -> p (b q) n", n=UNIT * H)

        in_x, in_edges, in_att, in_W, in_weights, in_small, in_scan = (
            sem("in_x"), sem("in_edges"), sem("in_att"), sem("in_W"), sem("in_weights"), sem("in_small"), sem("in_scan"))
        in_ends = sem("in_ends")
        dve_chain, pool_chain, act_chain = sem("dve_chain"), sem("pool_chain"), sem("act_chain")
        dve_mark, pool_mark = sem("dve_mark"), sem("pool_mark")
        consts_ready = sem("consts_ready")
        scan_read = sem("scan_read")
        x_pad = sem("x_pad")
        edges_ready = sem("edges_ready")
        edgesT_done, idx_ready = sem("edgesT_done"), sem("idx_ready")
        va_ready = sem("va_ready")
        xn_ready, xnT_done, xnT_ready, score_done, score_copied = (
            sem("xn_ready"), sem("xnT_done"), sem("xnT_ready"), sem("score_done"), sem("score_copied"))
        xn_stored = [sem(f"xn_stored{j}") for j in range(UNROLL)]
        tables_stored = sem("tables_stored")
        scan_pad = sem("scan_pad")
        idx_staged = sem("idx_staged")
        got = [sem(f"got{j}") for j in range(2)]
        rows_stored = [sem(f"rows_stored{j}") for j in range(2)]
        got_used = [sem(f"got_used{j}") for j in range(2)]
        lo_ready, loT_done, loT_ready = sem("lo_ready"), sem("loT_done"), sem("loT_ready")
        hi_done, hi_read = sem("hi_done"), sem("hi_read")
        edge_ready, edgeT_done, edge_copied = sem("edge_ready"), sem("edgeT_done"), sem("edge_copied")
        col_ready, row_done, row_ready, col_done = sem("col_ready"), sem("row_done"), sem("row_ready"), sem("col_done")
        exp_in, exp_out, scans_done = sem("exp_in"), sem("exp_out"), sem("scans_done")
        alpha_scan, alphaT_done, alpha_ready = sem("alpha_scan"), sem("alphaT_done"), sem("alpha_ready")
        home_row_ready, home_bc_done, step_cols_ready, step_row_done = (
            sem("home_row_ready"), sem("home_bc_done"), sem("step_cols_ready"), sem("step_row_done"))
        steps_ready = sem("steps_ready")
        rows_in = [sem(f"rows_in{j}") for j in range(G_RING // GROUP)]
        spread_ready, block_done, progress = sem("spread_ready"), sem("block_done"), sem("progress")
        diff_ready, hot_ready, extra_diff_ready = sem("diff_ready"), sem("hot_ready"), sem("extra_diff_ready")
        extra_hot_ready, extra_ready, extra_free = sem("extra_hot_ready"), sem("extra_ready"), sem("extra_free")
        carry_zero, carried, summed = sem("carry_zero"), sem("carried"), sem("summed")
        acc_free, acc_free2 = sem("acc_free"), sem("acc_free2")
        stage_out = [sem(f"stage_out{j}") for j in range(2)]
        bias_added = sem("bias_added")
        agg_in = [sem(f"agg_in{j}") for j in range(2)]
        proj_done, tn_ready, tr_done, tT_ready = sem("proj_done"), sem("tn_ready"), sem("tr_done"), sem("tT_ready")
        logit_done, shift_ready, exp_ready = sem("logit_done"), sem("shift_ready"), sem("exp_ready")
        comb_ready, combT_done, combT_ready, b2_done = (
            sem("comb_ready"), sem("combT_done"), sem("combT_ready"), sem("b2_done"))
        hT_done, h_ready, y_done, y_free = sem("hT_done"), sem("h_ready"), sem("y_done"), sem("y_free")
        out_stored = [sem(f"out_stored{j}") for j in range(2)]

        scan_dst = dst.rearrange("(c j) -> c j", c=CHUNKS)
        block = ctx.enter_context(nc.Block())

        @block.sync
        def _(sp):
            sp.dma_start(edges_i[0:CHUNKS, :], src.rearrange("(c j) -> c j", c=CHUNKS)).then_inc(in_edges, 16)
            sp.dma_start(edges_i[CHUNKS:, :], scan_dst).then_inc(in_edges, 16)
            sp.wait_ge(x_pad, 1)
            sp.dma_start(x_all[:, 0:FULL, :], x[0:FULL * P, :].rearrange("(t p) d -> p t d", p=P)).then_inc(in_x, 16)
            sp.dma_start(x_all[0:LAST, FULL, :], x[FULL * P:N, :]).then_inc(in_x, 16)
            sp.dma_start(W_sb[:, :, :], W.rearrange("(k p) n -> p k n", p=P)).then_inc(in_W, 16)
            for a, att in enumerate((att_src, att_dst)):
                sp.dma_start(att_bc[:, a, :], att.rearrange("h c -> (h c)").partition_broadcast(P)).then_inc(in_att, 16)
            for row, at in ((first_i, 0), (last_i, BLK - 1)):
                sp.dma_start(row[:, :], dst.rearrange("(a b j) -> a b j", a=1, j=BLK)[:, :, at],
                             allow_slow_non_contiguous=True).then_inc(in_ends, 16)
            sp.dma_start(bias_bc[:, :], gnn_bias.partition_broadcast(P)).then_inc(in_small, 16)
            sp.dma_start(b2_sb[:, :], b2).then_inc(in_small, 16)
            for k in range(2):
                sp.dma_start(router_sb[:, k, :], router_w[:, k * P:(k + 1) * P].rearrange("e p -> p e"),
                             allow_slow_non_contiguous=True).then_inc(in_small, 16)
                sp.dma_start(b1_sb[:, :, k], b1[:, k * P:(k + 1) * P].rearrange("e p -> p e"),
                             allow_slow_non_contiguous=True).then_inc(in_small, 16)
            sp.wait_ge(scan_pad, 2)
            for h in range(H):
                r = h * CHUNKS
                sp.dma_start(dst_scan_i[r:r + CHUNKS, 1:EC + 1], scan_dst).then_inc(in_scan, 16)
                sp.dma_start(dst_scan_i[r + 1:r + CHUNKS, 0:1], scan_dst[0:CHUNKS - 1, EC - 1:EC],
                             allow_slow_non_contiguous=True).then_inc(in_scan, 16)
                sp.dma_start(dst_scan_i[r:r + CHUNKS - 1, EC + 1:EC + 2], scan_dst[1:CHUNKS, 0:1],
                             allow_slow_non_contiguous=True).then_inc(in_scan, 16)
            with sp.Fori(0, TILES // UNROLL) as i:
                for j in range(UNROLL):
                    sp.wait_ge(xn_ready, i * UNROLL + (j + 1))
                    sp.dma_start(node_table[:, 0:D].rearrange("(t p) d -> t p d", p=P)[bass.ds(i * UNROLL + j, 1), :, :]
                                 .rearrange("t p d -> (t p) d"), xn[j][:, :]).then_inc(xn_stored[j], 16)
            sp.wait_ge(score_copied, TILES)
            sp.dma_start(node_table[:, D:].rearrange("(t p) h -> p t h", p=P), score_all[:, :, 0:H]).then_inc(tables_stored, 16)
            with sp.Fori(0, KB) as k:
                for j in range(2):
                    sp.wait_ge(got[j], k * (16 * HALF) + 16 * HALF)
                    sp.dma_start(edge_rows.rearrange("c k p d -> k p c d")[bass.ds(k, 1), :, j * HALF:(j + 1) * HALF, :]
                                 .rearrange("k p c d -> (k p) c d"), got_rows[j][:, :, 0:D]).then_inc(rows_stored[j], 16)
            for j in range(2):
                sp.wait_ge(rows_stored[j], 16 * KB)
            sp.wait_ge(scans_done, 1)
            blocks = edge_rows.rearrange("c k p d -> p (c k) d")
            for g in range(G_RING // GROUP):
                sp.dma_start(rows[:, g * GROUP:(g + 1) * GROUP, :], blocks[:, g * GROUP:(g + 1) * GROUP, :])\
                    .then_inc(rows_in[g], 16)
            for e in range(NX):
                sp.dma_start(w1_sb[:, e, :, :], w1[e].rearrange("(k p) n -> p k n", p=P)).then_inc(in_weights, 16)
                sp.dma_start(w2_sb[:, e, :, :], w2[e].rearrange("(k p) n -> p k n", p=P)).then_inc(in_weights, 16)
            with sp.Fori(0, NB // G_RING - 1) as i:
                for g in range(G_RING // GROUP):
                    sp.wait_ge(block_done, i * G_RING + (G_RING + (g + 1) * GROUP))
                    sp.dma_start(rows[:, g * GROUP:(g + 1) * GROUP, :],
                                 blocks[:, bass.ds(i * G_RING + (G_RING + g * GROUP), GROUP), :]).then_inc(rows_in[g], 16)

            def load_agg(j, n):
                sp.wait_ge(stage_out[j], (n + 1) * 16)
                sp.dma_start(aggt[j].rearrange("p m n -> p (m n)"),
                             agg_table[bass.ds(n * 2 + j, 1), :, :].rearrange("t p n -> (t p) n")).then_inc(agg_in[j], 16)

            def store_out(j, n):
                sp.wait_ge(y_free, (n * 2 + (j + 1)) * NX + 3)
                sp.dma_start(out[bass.ds((n * 2 + j) * P, P), :], res[j][:, :]).then_inc(out_stored[j], 16)

            load_agg(0, 0)
            load_agg(1, 0)
            with sp.Fori(0, TILES // 2 - 1) as i:
                for j in range(2):
                    sp.wait_ge(proj_done, i * 2 + (j + 1))
                    load_agg(j, i + 1)
                for j in range(2):
                    store_out(j, i)
            last = TILES // 2
            sp.wait_ge(proj_done, TILES - 2)
            load_agg(0, last)
            store_out(0, last - 1)
            store_out(1, last - 1)
            sp.wait_ge(y_free, TILES * NX + 3)
            sp.dma_start(out[FULL * P:N, :], res[0][0:LAST, :]).then_inc(out_stored[0], 16)
            sp.wait_ge(out_stored[0], 16 * (last + 1))
            sp.wait_ge(out_stored[1], 16 * last)

        @block.gpsimd
        def _(pool):
            count = [0]

            def link(ins):
                count[0] += 1
                ins.then_inc(pool_chain, 1)
                pool.wait_ge(pool_chain, count[0])

            pool.memset(x_all[:, FULL, :], 0.0).then_inc(x_pad, 1)
            link(pool.memset(ident[:, :], 0.0))
            pool.affine_select(out=ident[:, :], in_=ident[:, :], compare_op=ALU.not_equal, fill=1.0, base=0,
                               pattern=[[-1, P]], channel_multiplier=1).then_inc(consts_ready, 1)
            link(pool.iota(expert_ids_i[:, :], pattern=[[1, NX]], base=0, channel_multiplier=0))
            pool.tensor_copy(expert_ids[:, :], expert_ids_i[:, :]).then_inc(consts_ready, 1)
            link(pool.iota(home_ids_i[:, :], pattern=[[0, 1]], base=0, channel_multiplier=1))
            pool.tensor_copy(home_ids[:, :], home_ids_i[:, :]).then_inc(consts_ready, 1)
            HALF_IDS = TILES * P // 2
            for n in range(2):
                link(pool.iota(ids_i[:, 0:HALF_IDS], pattern=[[1, HALF_IDS]], base=n * HALF_IDS, channel_multiplier=0))
                link(pool.tensor_copy(node_ids[:, n * HALF_IDS:(n + 1) * HALF_IDS], ids_i[:, 0:HALF_IDS]))
            pool.memset(dst_scan_i[:, 0:1], -1).then_inc(scan_pad, 1)
            pool.memset(dst_scan_i[:, EC + 1:EC + 2], -1).then_inc(scan_pad, 1)

            pool.wait_ge(idx_ready, 1)
            pool.wait_ge(tables_stored, 16)
            for j in range(UNROLL):
                pool.wait_ge(xn_stored[j], 16 * (TILES // UNROLL))
            pool.wait_ge(scan_read, 1)
            with pool.Fori(0, KB) as k:
                for j in range(2):
                    pool.wait_ge(rows_stored[j], k * 16)
                    pool.wait_ge(got_used[j], k)
                    pool.tensor_copy(idx_stage[j][:, :].unsqueeze(1), src_k[:, bass.ds(k, 1), j * HALF:(j + 1) * HALF])\
                        .then_inc(idx_staged, 1)
                    pool.wait_ge(idx_staged, k * 2 + (j + 1))
                    pool.sem_inc(pool_mark, 1)
                    for c in range(HALF):
                        pool.indirect_dma_start(got_rows[j][:, c, :], None, node_table,
                                                bass.IndirectOffsetOnAxis(idx_stage[j][:, c:c + 1], 0)).then_inc(got[j], 16)
            pool.wait_ge(in_small, 16 * 6)
            with pool.Fori(0, TILES) as t:
                pool.tensor_tensor(x_all[:, bass.ds(t, 1), :], x_all[:, bass.ds(t, 1), :], bias_bc[:, :].unsqueeze(1), ALU.add)\
                    .then_inc(bias_added, 1)

            pool.wait_ge(alpha_ready, KB)
            pool.sem_inc(spread_ready, A_RING)

            def alphas(b, blocks, width):
                return alpha[:, bass.ds(b, blocks), :].unsqueeze(2).to_broadcast([BLK, blocks, width, H])

            def spread_blocks(b, slot, blocks, blocks_done):
                at = pool.value_load(home[0:1, bass.ds(b + (blocks - 1), 1)], min_val=0, max_val=NS - 1)
                pool.wait_ge(spread_ready, b + blocks)
                pool.tensor_tensor(hot[:, slot:slot + blocks, :],
                                   node_ids[0:BLK, 0:SPREAD].unsqueeze(1).to_broadcast([BLK, blocks, SPREAD]),
                                   dst_rel[:, bass.ds(b, blocks)].unsqueeze(2).to_broadcast([BLK, blocks, SPREAD]),
                                   ALU.subtract).then_inc(diff_ready, blocks)
                pool.wait_ge(diff_ready, b + blocks)
                pool.sem_inc(pool_mark, 1)
                pool.tensor_single_scalar(hot[:, slot:slot + blocks, :], hot[:, slot:slot + blocks, :], 0.0,
                                          op=ALU.is_equal).then_inc(hot_ready, blocks)
                pool.wait_ge(block_done, blocks_done)
                pool.wait_ge(acc_free, at + 1)
                pool.wait_ge(acc_free2, at + 1)
                pool.wait_ge(hot_ready, b + blocks)
                pool.tensor_tensor(
                    spread[:, slot:slot + blocks, :].rearrange("p s (d h) -> p s d h", h=H),
                    hot[:, slot:slot + blocks, :].unsqueeze(3).to_broadcast([BLK, blocks, SPREAD, H]),
                    alphas(b, blocks, SPREAD), ALU.mult).then_inc(spread_ready, blocks)
                return at

            with pool.Fori(0, NB // G_RING) as i:
                is_far = pool.value_load(far[0:1, bass.ds(i, 1)], min_val=0, max_val=2 * NS)
                with pool.If(is_far < 1):
                    for g in range(G_RING // GROUP):
                        b = i * G_RING + g * GROUP
                        spread_blocks(b, g * GROUP % A_RING, GROUP, b + (GROUP - 1 + 1 + G_RING - A_RING))
                with pool.Else():
                    for slot in range(G_RING):
                        b = i * G_RING + slot
                        at = spread_blocks(b, slot % A_RING, 1, b + (1 + G_RING - A_RING))
                        more = pool.value_load(extras[0:1, bass.ds(b, 1)], min_val=0, max_val=NS)
                        before = pool.value_load(extra_before[0:1, bass.ds(b, 1)], min_val=0, max_val=NB + NS)
                        with pool.If(more > 0):
                            with pool.Fori(0, more) as d:
                                n = before + d
                                pool.wait_ge(extra_free, n + 1)
                                pool.wait_ge(extra_ready, n)
                                to = pool.snap((at + d) % NS)
                                pool.tensor_tensor(
                                    extra_hot, node_ids[0:BLK, bass.ds(to * HOME, HOME)].unsqueeze(1),
                                    dst_far[:, bass.ds(b, 1)].unsqueeze(2).to_broadcast([BLK, 1, HOME]),
                                    ALU.subtract).then_inc(extra_diff_ready, 1)
                                pool.wait_ge(extra_diff_ready, n + 1)
                                pool.sem_inc(pool_mark, 1)
                                pool.tensor_single_scalar(extra_hot, extra_hot, 0.0, op=ALU.is_equal)\
                                    .then_inc(extra_hot_ready, 1)
                                pool.wait_ge(extra_hot_ready, n + 1)
                                pool.wait_ge(acc_free, at + d + 1)
                                pool.wait_ge(acc_free2, at + d + 1)
                                pool.tensor_tensor(
                                    extra[:, bass.ds(n % 2, 1), :].rearrange("p o (d h) -> p o d h", h=H),
                                    extra_hot.unsqueeze(3).to_broadcast([BLK, 1, HOME, H]),
                                    alphas(b, 1, HOME), ALU.mult).then_inc(extra_ready, 1)

        @block.tensor
        def _(pe):
            pe.wait_ge(consts_ready, 2)
            pe.wait_ge(edges_ready, 1)
            for k in range(KB):
                m = pe.transpose(bank[k // 16][0:BLK, (k % 16) * 32:(k % 16) * 32 + 32],
                                 edges_f[:, k * BLK:(k + 1) * BLK], ident[0:32, 0:32])
            m.then_inc(edgesT_done, 1)
            pe.wait_ge(va_ready, 1)
            with pe.Fori(0, TILES // UNROLL) as i:
                for j in range(UNROLL):
                    pe.wait_ge(xn_ready, i * UNROLL + (j + 1))
                    pe.wait_ge(score_copied, i * UNROLL)
                    pe.transpose(bank[2 + j][:, 0:P], xn[j][:, 0:P], ident[:, :])
                    pe.transpose(bank[2 + j][:, P:D], xn[j][:, P:D], ident[:, :]).then_inc(xnT_done, 1)
                for j in range(UNROLL):
                    pe.wait_ge(xnT_ready, i * UNROLL + (j + 1))
                    for k in range(2):
                        m = pe.matmul(bank[2 + j][:, D:D + 2 * H], xnT[j][:, k * P:(k + 1) * P], va[:, k, :],
                                      start=(k == 0), stop=(k == 1))
                    m.then_inc(score_done, 1)
            pe.wait_ge(home_row_ready, 1)
            for to, row in ((0, first_f), (1, home_f), (7, last_home_f)):
                m = pe.matmul(bank[to][:, 0:NB], ones_row[0:1, :], row[0:1, :], start=True, stop=True)
            m.then_inc(home_bc_done, 1)
            pe.wait_ge(step_cols_ready, 1)
            pe.transpose(bank[1][0:1, 0:P], step_cols[:, 0:1], ident[:, :]).then_inc(step_row_done, 1)
            pe.wait_ge(steps_ready, 1)
            pe.wait_ge(score_copied, TILES)

            def turn_lo(j, n):
                pe.wait_ge(lo_ready, n + 1)
                pe.wait_ge(loT_ready, n)
                for c in range(HALF):
                    m = pe.transpose(bank[c // 4][:, (c % 4) * P:(c % 4) * P + BLK], lo_hot[:, c, :], ident[0:BLK, 0:BLK])
                m.then_inc(loT_done, 1)

            def pick_lo(j, n):
                pe.wait_ge(loT_ready, n + 1)
                pe.wait_ge(hi_read, n)
                for c in range(HALF):
                    m = pe.matmul(bank[2 + c // 2][0:BLK, (c % 2) * TILES * H:(c % 2 + 1) * TILES * H],
                                  lo_hotT[j][:, c * BLK:(c + 1) * BLK], score_all[:, :, H:2 * H], start=True, stop=True)
                m.then_inc(hi_done, 1)

            for j in range(2):
                turn_lo(j, j)
                pick_lo(j, j)
            with pe.Fori(0, KB) as k:
                for j in range(2):
                    turn_lo(j, k * 2 + (j + 2))
                    pick_lo(j, k * 2 + (j + 2))
                pe.wait_ge(edge_ready, k + 1)
                pe.wait_ge(edge_copied, k)
                pe.transpose(bank[7][:, 0:BLK], edge_e[:, :], ident[0:BLK, 0:BLK]).then_inc(edgeT_done, 1)
            for n in range(4):
                pe.wait_ge(col_ready, n + 1)
                pe.transpose(bank[0][0:1, 0:P], cols[:, 0:1], ident[:, :])
                pe.transpose(bank[0][0:1, P:2 * P], cols[:, 1:2], ident[:, :]).then_inc(row_done, 1)
                pe.wait_ge(row_ready, n + 1)
                pe.transpose(bank[1][:, 0:1], chain_rows[0:1, 3 * P + 1 + n % 2:4 * P + 1 + n % 2],
                             ident[0:1, 0:1]).then_inc(col_done, 1)
            for k in range(KB):
                if k % (KB // UNROLL) == 0:
                    pe.wait_ge(alpha_scan, k // (KB // UNROLL) + 1)
                if k >= 4:
                    pe.wait_ge(alpha_ready, k - 3)
                pe.transpose(bank[4 + k % 4][0:BLK, 0:P], buf_E[:, k * BLK:(k + 1) * BLK], ident[:, :])\
                    .then_inc(alphaT_done, 1)

            pe.wait_ge(alpha_ready, KB)
            pe.sem_inc(block_done, G_RING - 1)
            pe.sem_inc(extra_free, 2)

            def add_block(at, slot):
                for k in range(2):
                    m = pe.matmul(units[:, bass.ds(at + k * BANK, SPREAD // UNIT), :],
                                  rows[0:BLK, slot, k * P:(k + 1) * P],
                                  spread[:, slot % A_RING, :].rearrange("p (q n) -> p q n", n=UNIT * H),
                                  start=False, stop=True, skip_group_check=True)
                    m.then_inc(progress if k else block_done, 1)

            words = places[0:1, :].bitcast(I32)
            with pe.Fori(0, NB // G_RING) as i:
                is_far = pe.value_load(far[0:1, bass.ds(i, 1)], min_val=0, max_val=2 * NS)
                with pe.If(is_far < 1):
                    for g in range(G_RING // GROUP):
                        word = pe.value_load(words[0:1, bass.ds(i * (G_RING // GROUP) + g, 1)], min_val=0, max_val=2 ** 31 - 1)
                        pe.wait_ge(rows_in[g], i * 16 + 16)
                        pe.wait_ge(spread_ready, i * G_RING + ((g + 1) * GROUP + A_RING))
                        for s in range(GROUP):
                            add_block(nc.s_assert_within(
                                (word // 256 ** s) % 128, 0, MAX_PLACE,
                                skip_runtime_bounds_check_because="a byte of places is 32 * (home % 4) + less than 8"),
                                g * GROUP + s)
                with pe.Else():
                    for slot in range(G_RING):
                        b = i * G_RING + slot
                        if slot % GROUP == 0:
                            pe.wait_ge(rows_in[slot // GROUP], i * 16 + 16)
                        at = pe.value_load(place[0:1, bass.ds(b, 1)], min_val=0, max_val=MAX_PLACE)
                        pe.wait_ge(spread_ready, b + (1 + A_RING))
                        add_block(at, slot)
                        more = pe.value_load(extras[0:1, bass.ds(b, 1)], min_val=0, max_val=NS)
                        before = pe.value_load(extra_before[0:1, bass.ds(b, 1)], min_val=0, max_val=NB + NS)
                        start = pe.value_load(home[0:1, bass.ds(b, 1)], min_val=0, max_val=NS - 1)
                        with pe.If(more > 0):
                            with pe.Fori(0, more) as d:
                                n = before + d
                                pe.wait_ge(extra_ready, n + 1)
                                for k in range(2):
                                    m = pe.matmul(banks[:, bass.ds((start + d) % ACC_RING * 2 + k, 1), 0:HOME * H],
                                                  rows[0:BLK, slot, k * P:(k + 1) * P], extra[:, bass.ds(n % 2, 1), :],
                                                  start=False, stop=True, skip_group_check=True)
                                m.then_inc(extra_free, 1)
                                pe.drain().then_inc(progress, 1)

            pe.wait_ge(acc_free, NS + 1)
            pe.wait_ge(acc_free2, NS + 1)

            def project(j, n):
                pe.wait_ge(agg_in[j], (n + 1) * 16)
                for k in range(2):
                    for h in range(H):
                        m = pe.matmul(bank[0][:, 0:C], aggt[j][:, k * H + h, :], W_sb[:, k, h * C:(h + 1) * C],
                                      start=(k == 0 and h == 0), stop=(k == 1 and h == H - 1))
                m.then_inc(proj_done, 1)

            def turn_tn(j, t):
                pe.wait_ge(tn_ready, t + 1)
                for k in range(2):
                    m = pe.transpose(bank[1][:, k * P:(k + 1) * P], tn[j][:, k * P:(k + 1) * P], ident[:, :])
                m.then_inc(tr_done, 1)

            def router(j, t):
                pe.wait_ge(tT_ready, t + 1)
                for k in range(2):
                    m = pe.matmul(bank[1][:, D:D + NX], tT[j][:, k, :], router_sb[:, k, :], start=(k == 0), stop=(k == 1))
                m.then_inc(logit_done, 1)

            def turn_comb(j, t):
                pe.wait_ge(comb_ready, t + 1)
                pe.transpose(bank[1][0:NX, 384:384 + P], comb[j][:, :], ident[:, :]).then_inc(combT_done, 1)

            def bias_mix(t):
                pe.wait_ge(combT_ready, t + 1)
                pe.matmul(bank[1][:, 0:D], combT[:, :], b2_sb[:, :], start=True, stop=True).then_inc(b2_done, 1)

            def up(j, e):
                for f in range(2):
                    for k in range(2):
                        m = pe.matmul(h_bank[e % 3][:, f * P:(f + 1) * P], w1_sb[:, e, k, f * P:(f + 1) * P],
                                      tT[j][:, k, :], start=(k == 0), stop=(k == 1))
                m.then_inc(hT_done, 1)

            def down(j, e, t):
                pe.wait_ge(h_ready, t * NX + (e + 1))
                pe.wait_ge(y_free, t * NX + ((2, 3, 1)[e] if e < 3 else e + 1))
                for f in range(2):
                    m = pe.matmul(y_bank[e % 3][:, 0:D], h_sb[e % 3][:, f, :], w2_sb[:, e, f, :],
                                  start=(f == 0), stop=(f == 1))
                m.then_inc(y_done, 1)

            def tile(j, n, ahead):
                t = n * 2 + j
                if ahead:
                    project(1 - j, n + j)
                for e in range(NX):
                    if ahead and e == 3:
                        turn_tn(1 - j, t + 1)
                    if e + 2 < NX:
                        up(j, e + 2)
                    if ahead and e == 3:
                        router(1 - j, t + 1)
                    down(j, e, t)
                    if ahead and e == NX - 2:
                        up(1 - j, 0)
                        turn_comb(1 - j, t + 1)
                if ahead:
                    bias_mix(t + 1)
                    up(1 - j, 1)

            project(0, 0)
            turn_tn(0, 0)
            router(0, 0)
            turn_comb(0, 0)
            bias_mix(0)
            pe.wait_ge(in_weights, 16 * 2 * NX)
            pe.wait_ge(acc_free, NS + ACC_RING)
            pe.wait_ge(acc_free2, NS + ACC_RING)
            up(0, 0)
            up(0, 1)
            with pe.Fori(0, TILES // 2) as i:
                tile(0, i, True)
                tile(1, i, True)
            tile(0, TILES // 2, False)

        @block.scalar
        def _(act):
            with act.Fori(0, TILES // UNROLL) as i:
                for j in range(UNROLL):
                    act.wait_ge(xnT_done, i * UNROLL + (j + 1))
                    act.copy(xnT[j][:, :], bank[2 + j][:, 0:D]).then_inc(xnT_ready, 1)
                for j in range(UNROLL):
                    act.wait_ge(score_done, i * UNROLL + (j + 1))
                    act.copy(score_all[:, bass.ds(i * UNROLL + j, 1), :], bank[2 + j][:, D:D + 2 * H].unsqueeze(1))\
                        .then_inc(score_copied, 1)
            def copy_lo(j, n):
                act.wait_ge(loT_done, n + 1)
                for q in range(2):
                    c = act.copy(lo_hotT[j][:, q * 4 * BLK:(q + 1) * 4 * BLK].rearrange("p (c n) -> p c n", c=4),
                                 bank[q].rearrange("p (c n) -> p c n", c=4)[:, :, 0:BLK])
                c.then_inc(loT_ready, 1)

            for j in range(2):
                copy_lo(j, j)
            with act.Fori(0, KB) as k:
                for j in range(2):
                    copy_lo(j, k * 2 + (j + 2))
                act.wait_ge(edgeT_done, k + 1)
                act.copy(buf_E[:, bass.ds(k * BLK, BLK)], bank[7][:, 0:BLK]).then_inc(edge_copied, 1)
            act.wait_ge(exp_in, 1)
            act.activation(buf_E[:, :], buf_E[:, :], ACT.Exp).then_inc(exp_out, 1)
            alpha_v = alpha[:, :, :].rearrange("p (c k) h -> p k h c", k=KB)
            for k in range(KB):
                act.wait_ge(alphaT_done, k + 1)
                act.copy(alpha_v[:, k, :, :], bank[4 + k % 4][0:BLK, 0:P].rearrange("p (h c) -> p h c", h=H))\
                    .then_inc(alpha_ready, 1)
            act.wait_ge(acc_free, ACC_RING)
            act.wait_ge(carry_zero, 1)

            def tile_out(j, n):
                for v in range(HOMES):
                    at = (n * 2 + j) * HOMES + v
                    last = act.value_load(steps_to[0:1, bass.ds(at, 1)], min_val=0, max_val=2 * NB + NS)
                    act.wait_ge(progress, last)
                    act.copy(carry[:, v % 2, :, 0:OVER, :], sums[:, v, :, HOME:SLOTS, :]).then_inc(carried, 1)
                    act.wait_ge(summed, at + 1)
                    act.copy(bank[2 * v][:, 0:SLOTS * H], zeros[:, 0:1].to_broadcast([P, SLOTS * H])).then_inc(acc_free, 1)
                act.dma_start(agg_table[bass.ds(n * 2 + j, 1), :, :].rearrange("t p n -> (t p) n"),
                              stage[j].rearrange("p m n -> p (m n)")).then_inc(stage_out[j], 16)

            with act.Fori(0, TILES // 2) as i:
                tile_out(0, i)
                tile_out(1, i)
            tile_out(0, TILES // 2)

            act.wait_ge(in_small, 16 * 6)

            def turn(j, t):
                act.wait_ge(tr_done, t + 1)
                act.copy(tT[j][:, :, :], bank[1][:, 0:D].rearrange("p (k n) -> p k n", k=2)).then_inc(tT_ready, 1)

            def route(j, t):
                act.wait_ge(shift_ready, t + 1)
                act.activation(small[j][:, 8:8 + NX], bank[1][:, D:D + NX], ACT.Exp, bias=small[j][:, 0:1],
                               accum_out=small[j][:, 1:2]).then_inc(exp_ready, 1)

            def mix(t):
                act.wait_ge(combT_done, t + 1)
                act.copy(combT[:, :], bank[1][0:NX, 384:384 + P]).then_inc(combT_ready, 1)

            def gelus(e, t):
                act.wait_ge(hT_done, t * NX + (e + 1))
                for f in range(2):
                    g = act.activation(h_sb[e % 3][:, f, :], h_bank[e % 3][:, f * P:(f + 1) * P], ACT.Gelu,
                                       bias=b1_sb[:, e, f:f + 1])
                g.then_inc(h_ready, 1)

            def tile(j, n, ahead):
                t = n * 2 + j
                for e in range(NX):
                    gelus(e, t)
                    if ahead and e == 3:
                        turn(1 - j, t + 1)
                    if ahead and e == 4:
                        route(1 - j, t + 1)
                if ahead:
                    mix(t + 1)

            turn(0, 0)
            route(0, 0)
            mix(0)
            with act.Fori(0, TILES // 2) as i:
                tile(0, i, True)
                tile(1, i, True)
            tile(0, TILES // 2, False)

        @block.vector
        def _(dve):
            count = [0]

            def link(ins):
                count[0] += 1
                ins.then_inc(dve_chain, 1)
                dve.wait_ge(dve_chain, count[0])

            link(dve.memset(zeros[:, :], 0.0))
            def inv_sqrt(chained, y, var, t, half_v):
                chained(dve.tensor_scalar(half_v, var, LN_EPS, None, ALU.add))
                chained(dve.tensor_single_scalar(t.bitcast(I32), half_v.bitcast(I32), 1, op=ALU.arith_shift_right))
                chained(dve.tensor_scalar(y.bitcast(I32), t.bitcast(I32), -1.0, RSQRT_MAGIC, ALU.mult, ALU.add))
                chained(dve.tensor_scalar(half_v, half_v, -0.5, None, ALU.mult))
                for _ in range(NEWTON_STEPS):
                    chained(dve.tensor_tensor(t, y, y, ALU.mult))
                    chained(dve.tensor_tensor(t, t, half_v, ALU.mult))
                    chained(dve.scalar_tensor_tensor(y, t, 1.5, y, ALU.add, ALU.mult))

            link(dve.memset(ones_row[:, :], 1.0))
            link(dve.memset(src_k[:, :, :], 0))
            link(dve.memset(dst_k[:, :, :], 0))
            dve.wait_ge(in_edges, 32)
            dve.tensor_copy(edges_f, edges_i).then_inc(edges_ready, 1)
            dve.wait_ge(in_x, 32)
            with dve.Fori(0, TILES) as t:
                dve.bn_stats(stats[:, bass.ds(t, 1), :].rearrange("p t s -> p (t s)"),
                             x_all[:, bass.ds(t, 1), :].rearrange("p t d -> p (t d)")).then_inc(dve_chain, 1)
            count[0] += TILES
            dve.wait_ge(dve_chain, count[0])
            link(dve.tensor_tensor(mean[:, :], stats[:, :, 1], stats[:, :, 4], ALU.add))
            link(dve.tensor_scalar(mean[:, :], mean[:, :], 0.5, None, ALU.mult))
            link(dve.tensor_tensor(half[:, :], stats[:, :, 1], stats[:, :, 4], ALU.subtract))
            link(dve.tensor_scalar(half[:, :], half[:, :], 0.5, None, ALU.mult))
            link(dve.tensor_tensor(half[:, :], half[:, :], half[:, :], ALU.mult))
            link(dve.tensor_tensor(rstd[:, :], stats[:, :, 2], stats[:, :, 5], ALU.add))
            link(dve.scalar_tensor_tensor(rstd[:, :], rstd[:, :], 1.0 / D, half[:, :], ALU.mult, ALU.add))
            inv_sqrt(link, rstd[:, :], rstd[:, :], half[:, :], inv_tmp[:, :])
            dve.wait_ge(in_att, 32)
            dve.wait_ge(in_W, 16)
            for a in range(2):
                for k in range(2):
                    for h in range(H):
                        link(dve.tensor_tensor_reduce(out=att_junk, in0=W_sb[:, k, h * C:(h + 1) * C],
                                                      in1=att_bc[:, a, h * C:(h + 1) * C], scale=1.0, scalar=0.0,
                                                      op0=ALU.mult, op1=ALU.add,
                                                      accum_out=va[:, k, a * H + h:a * H + h + 1]))
            dve.sem_inc(va_ready, 1)
            with dve.Fori(0, TILES // UNROLL) as i:
                for j in range(UNROLL):
                    dve.wait_ge(xn_stored[j], i * 16)
                    dve.wait_ge(xnT_done, i * UNROLL)
                    dve.tensor_scalar(xn[j][:, :].unsqueeze(1), x_all[:, bass.ds(i * UNROLL + j, 1), :],
                                      mean[:, bass.ds(i * UNROLL + j, 1)], rstd[:, bass.ds(i * UNROLL + j, 1)],
                                      ALU.subtract, ALU.mult).then_inc(xn_ready, 1)
            dve.wait_ge(edgesT_done, 1)
            for n, (k0, k1) in enumerate(((0, 16), (16, KB))):
                v = bank[n][0:BLK, 0:(k1 - k0) * 32].rearrange("p (k c) -> p k c", c=32)
                link(dve.tensor_copy(dst_f[:, :].rearrange("p (c k) -> p k c", k=KB)[:, k0:k1, :], v[:, :, CHUNKS:]))
                link(dve.tensor_copy(dst_k[:, k0:k1, :], v[:, :, CHUNKS:]))
                link(dve.tensor_copy(src_k[0:BLK, k0:k1, :], v[:, :, 0:CHUNKS]))
            dve.sem_inc(idx_ready, 1)
            link(dve.tensor_single_scalar(dst_hi[:, :, :].bitcast(I32), dst_k[:, :, :], 7, op=ALU.arith_shift_right))
            link(dve.tensor_single_scalar(dst_k[:, :, :], dst_k[:, :, :], P - 1, op=ALU.bitwise_and))
            link(dve.tensor_copy(dst_lo[:, :, :], dst_k[:, :, :]))
            link(dve.tensor_copy(dst_k[:, :, :], dst_hi[:, :, :].bitcast(I32)))
            link(dve.tensor_copy(dst_hi[:, :, :], dst_k[:, :, :]))
            dve.wait_ge(in_ends, 32)
            link(dve.tensor_single_scalar(row_tmp[:, :], first_i[:, :], ACC_RING * HOME - 1, op=ALU.bitwise_and))
            link(dve.tensor_single_scalar(row_tmp[:, :], row_tmp[:, :], 2, op=ALU.arith_shift_right))
            link(dve.tensor_single_scalar(place[:, :], row_tmp[:, :], (ACC_RING - 1) * (HOME // UNIT), op=ALU.bitwise_and))
            link(dve.scalar_tensor_tensor(place[:, :], place[:, :], float(2 * BANK // (HOME // UNIT) - 1), row_tmp[:, :],
                                          ALU.mult, ALU.add))
            link(dve.tensor_copy(places[:, :], place[:, :]))
            link(dve.tensor_single_scalar(home[:, :], first_i[:, :], 5, op=ALU.arith_shift_right))
            link(dve.tensor_copy(home_f[:, :], home[:, :]))
            link(dve.tensor_single_scalar(row_tmp[:, :], last_i[:, :], 5, op=ALU.arith_shift_right))
            link(dve.tensor_copy(last_home_f[:, :], row_tmp[:, :]))
            link(dve.tensor_single_scalar(row_tmp[:, :], first_i[:, :], -UNIT, op=ALU.bitwise_and))
            link(dve.tensor_copy(first_f[:, :], row_tmp[:, :]))
            link(dve.tensor_copy(extra_f[:, :], last_i[:, :]))
            link(dve.tensor_tensor(extra_f[:, :], extra_f[:, :], first_f[:, :], ALU.subtract))
            link(dve.tensor_scalar(extra_f[:, :], extra_f[:, :], float(SPREAD), None, ALU.is_ge))
            link(dve.tensor_tensor(last_home_f[:, :], last_home_f[:, :], home_f[:, :], ALU.subtract))
            link(dve.scalar_tensor_tensor(extra_f[:, :], last_home_f[:, :], 1.0, extra_f[:, :], ALU.add, ALU.mult))
            link(dve.scalar_tensor_tensor(last_home_f[:, :], extra_f[:, :], -1.0, home_f[:, :], ALU.add, ALU.add))
            dve.sem_inc(home_row_ready, 1)
            link(dve.tensor_copy(extras[:, :], extra_f[:, :]))
            link(dve.memset(extra_sum[:, 0:1], 0.0))
            link(dve.tensor_tensor_scan(extra_sum[:, 1:NB + 1], extra_f[:, :], extra_f[:, :], 0.0, ALU.add, ALU.bypass))
            link(dve.tensor_copy(extra_before[:, :], extra_sum[:, :]))
            homes_g = home_f[:, :].rearrange("p (g b) -> p g b", b=GROUP)
            link(dve.tensor_tensor(span_f[:, :], homes_g[:, :, GROUP - 1], homes_g[:, :, 0], ALU.subtract))
            link(dve.tensor_scalar(span_f[:, :], span_f[:, :], float(ACC_RING), None, ALU.is_ge))
            link(dve.tensor_reduce(far_f[:, 0, :], span_f[:, :].rearrange("p (i g) -> p i g", g=G_RING // GROUP), AX_X, ALU.max))
            link(dve.tensor_reduce(far_f[:, 1, :], extra_f[:, :].rearrange("p (i b) -> p i b", b=G_RING), AX_X, ALU.max))
            link(dve.tensor_tensor(far_f[:, 0, :], far_f[:, 0, :], far_f[:, 1, :], ALU.add))
            link(dve.tensor_copy(far[:, :], far_f[:, 0, :]))
            dve.wait_ge(consts_ready, 3)
            dve.wait_ge(home_bc_done, 1)
            link(dve.scalar_tensor_tensor(dst_rel[:, :], bank[0][0:BLK, 0:NB], -1.0, dst_f[:, :], ALU.mult, ALU.add))
            link(dve.tensor_scalar(reach_junk[0:BLK, :], dst_rel[:, :], float(SPREAD), None, ALU.is_ge))
            link(dve.scalar_tensor_tensor(dst_far[:, :], dst_f[:, :], 1.0, reach_junk[0:BLK, :], ALU.add, ALU.mult))
            link(dve.tensor_scalar(dst_far[:, :], dst_far[:, :], 1.0, None, ALU.subtract))
            link(dve.tensor_copy(first_home_bc, bank[1][:, 0:NB]))
            link(dve.tensor_copy(last_home_bc, bank[7][:, 0:NB]))
            link(dve.tensor_scalar(reach_junk, first_home_bc, home_ids[:, 0:1], None, ALU.is_le))
            link(dve.tensor_reduce(step_cols[:, 0:1], reach_junk, AX_X, ALU.add))
            link(dve.scalar_tensor_tensor(reach_junk, last_home_bc, home_ids[:, 0:1], first_home_bc, ALU.min, ALU.subtract))
            link(dve.tensor_scalar(reach_junk, reach_junk, 1.0, 0.0, ALU.add, ALU.max))
            link(dve.tensor_reduce(step_cols[:, 1:2], reach_junk, AX_X, ALU.add))
            link(dve.tensor_tensor(step_cols[:, 0:1], step_cols[:, 0:1], step_cols[:, 1:2], ALU.add))
            dve.sem_inc(step_cols_ready, 1)
            dve.wait_ge(step_row_done, 1)
            dve.tensor_copy(steps_to[:, :], bank[1][0:1, 0:P]).then_inc(steps_ready, 1)
            dve.wait_ge(in_scan, 16 * 3 * H)
            link(dve.tensor_copy(dst_scan_f, dst_scan_i))
            link(dve.tensor_tensor(buf_keep, dst_scan_f[:, 0:EC + 1], dst_scan_f[:, 1:EC + 2], ALU.is_equal))
            dve.sem_inc(scan_read, 1)
            link(dve.tensor_scalar(buf_reset, buf_keep, 1.0, BIG, ALU.subtract, ALU.mult))
            link(dve.tensor_reduce(cols[:, 2:3], buf_keep[:, 0:EC], AX_X, ALU.min))
            link(dve.tensor_reduce(cols[:, 3:4], buf_keep[:, 1:EC + 1], AX_X, ALU.min))
            link(dve.tensor_scalar(cols[:, 4:6], cols[:, 2:4], 1.0, BIG, ALU.subtract, ALU.mult))
            def one_hot_lo(k, j, n):
                dve.wait_ge(loT_done, n)
                dve.tensor_tensor(lo_hot[:, :, :], node_ids[0:BLK, 0:P].unsqueeze(1).to_broadcast([BLK, HALF, P]),
                                  dst_lo[:, bass.ds(k, 1), j * HALF:(j + 1) * HALF].rearrange("p o c -> p (o c)")
                                  .unsqueeze(2).to_broadcast([BLK, HALF, P]), ALU.is_equal).then_inc(lo_ready, 1)

            def pick_hi(k, j, l):
                l(dve.tensor_tensor(hi_hot[:, :, :], node_ids[0:BLK, 0:TILES].unsqueeze(1).to_broadcast([BLK, HALF, TILES]),
                                    dst_hi[:, bass.ds(k, 1), j * HALF:(j + 1) * HALF].rearrange("p o c -> p (o c)")
                                    .unsqueeze(2).to_broadcast([BLK, HALF, TILES]), ALU.is_equal))
                dve.wait_ge(hi_done, k * 2 + (j + 1))
                for q in range(HALF // 2):
                    m = dve.tensor_tensor(
                        hi_picked[:, 2 * q:2 * q + 2, :].rearrange("p c (t h) -> p c t h", h=H),
                        bank[2 + q][0:BLK, 0:2 * TILES * H].rearrange("p (c t h) -> p c t h", c=2, h=H),
                        hi_hot[:, 2 * q:2 * q + 2, :].unsqueeze(3).to_broadcast([BLK, 2, TILES, H]), ALU.mult)
                m.then_inc(hi_read, 1)
                dve.wait_ge(hi_read, k * 2 + (j + 1))
                l(dve.tensor_reduce(score_d[j][:, :, :], hi_picked[:, :, :].rearrange("p c (t h) -> p c h t", h=H),
                                    AX_X, ALU.add))

            def edge_score(k, j, l):
                dve.wait_ge(got[j], k * (16 * HALF) + 16 * HALF)
                dve.tensor_tensor(edge_z[:, :, :], got_rows[j][0:BLK, :, D:ROW], score_d[j][:, :, :], ALU.add)\
                    .then_inc(got_used[j], 1)
                dve.wait_ge(got_used[j], k + 1)
                if j == 0:
                    dve.wait_ge(edgeT_done, k)
                l(dve.scalar_tensor_tensor(
                    edge_e[:, :].rearrange("p (h c) -> p c h", h=H)[:, j * HALF:(j + 1) * HALF, :], edge_z[:, :, :],
                    NEG_SLOPE, edge_z[:, :, :], ALU.mult, ALU.max))

            one_hot_lo(0, 0, 0)
            one_hot_lo(0, 1, 1)
            pick_hi(0, 0, link)
            base = count[0]
            with dve.Fori(0, KB) as k:
                at = [0]

                def link_k(ins):
                    at[0] += 1
                    ins.then_inc(dve_chain, 1)
                    dve.wait_ge(dve_chain, k * STAGE2_LINKS + (base + at[0]))

                one_hot_lo(k + 1, 0, k * 2 + 2)
                pick_hi(k, 1, link_k)
                edge_score(k, 0, link_k)
                one_hot_lo(k + 1, 1, k * 2 + 3)
                pick_hi(k + 1, 0, link_k)
                edge_score(k, 1, link_k)
                dve.sem_inc(edge_ready, 1)
                assert at[0] == STAGE2_LINKS
            count[0] += KB * STAGE2_LINKS
            dve.wait_ge(edge_copied, KB)
            for j in range(2):
                dve.wait_ge(rows_stored[j], 16 * KB)

            turn = [0]

            def chained_scan(res_v, data0, data1, all_keep, op0, op1, init, back):
                n = turn[0]
                turn[0] += 1
                r = (lambda a: a[:, ::-1]) if back else (lambda a: a)
                end = res_v[:, 0:1] if back else res_v[:, EC - 1:EC]
                link(dve.tensor_tensor_scan(r(res_v), r(data0), r(data1), init, op0, op1))
                link(dve.tensor_copy(cols[:, 1:2], all_keep))
                dve.tensor_copy(cols[:, 0:1], end).then_inc(col_ready, 1)
                dve.wait_ge(row_done, n + 1)
                link(dve.tensor_copy(chain_rows[0:1, 0:2 * P], bank[0][0:1, 0:2 * P]))
                vals, keeps = chain_rows[0:1, 0:P], chain_rows[0:1, P:2 * P]
                shifted = chain_rows[0:1, 3 * P + 1 + n % 2:4 * P + 1 + n % 2]
                link(dve.memset(chain_rows[0:1, 3 * P:4 * P + 4], init))
                outs = chain_rows[0:1, 2 * P:3 * P]
                link(dve.tensor_tensor_scan(r(outs), r(keeps), r(vals), init, op0, op1))
                if back:
                    dve.tensor_copy(shifted[:, 0:P - 1], outs[:, 1:P]).then_inc(row_ready, 1)
                else:
                    dve.tensor_copy(shifted[:, 1:P], outs[:, 0:P - 1]).then_inc(row_ready, 1)
                dve.wait_ge(col_done, n + 1)
                link(dve.tensor_copy(cols[:, 6:7], bank[1][:, 0:1]))
                link(dve.tensor_tensor_scan(r(res_v), r(data0), r(data1), cols[:, 6:7], op0, op1))

            chained_scan(buf_F, buf_reset[:, 0:EC], buf_E, cols[:, 4:5], ALU.add, ALU.max, -BIG, False)
            chained_scan(buf_B, buf_reset[:, 1:EC + 1], buf_E, cols[:, 5:6], ALU.add, ALU.max, -BIG, True)
            link(dve.tensor_tensor(buf_F, buf_F, buf_B, ALU.max))
            dve.tensor_tensor(buf_E, buf_E, buf_F, ALU.subtract).then_inc(exp_in, 1)
            dve.wait_ge(exp_out, 1)
            chained_scan(buf_F, buf_keep[:, 0:EC], buf_E, cols[:, 2:3], ALU.mult, ALU.add, 0.0, False)
            chained_scan(buf_B, buf_keep[:, 1:EC + 1], buf_E, cols[:, 3:4], ALU.mult, ALU.add, 0.0, True)
            dve.sem_inc(scans_done, 1)
            link(dve.tensor_tensor(buf_B, buf_B, buf_E, ALU.subtract))
            link(dve.scalar_tensor_tensor(buf_F, buf_F, SOFTMAX_EPS, buf_B, ALU.add, ALU.add))
            for n in range(UNROLL):
                piece = slice(n * (EC // UNROLL), (n + 1) * (EC // UNROLL))
                link(dve.reciprocal(buf_F[:, piece], buf_F[:, piece]))
                dve.tensor_tensor(buf_E[:, piece], buf_E[:, piece], buf_F[:, piece], ALU.mult).then_inc(alpha_scan, 1)

            dve.memset(ring1[:, 0:4 * HOME * H], 0.0).then_inc(carry_zero, 1)
            for r in range(ACC_RING):
                if r == 2:
                    dve.wait_ge(alpha_ready, KB)
                dve.memset(bank[2 * r][:, :], 0.0).then_inc(acc_free, 1)
                dve.memset(bank[2 * r + 1][:, :], 0.0).then_inc(acc_free2, 1)

            def tile_sums(j, n):
                dve.wait_ge(stage_out[j], n * 16)
                for v in range(HOMES):
                    dve.wait_ge(carried, (n * 2 + j) * HOMES + (v + 1))
                    dve.tensor_tensor(stage[j].rearrange("p (k h) n -> p k n h", k=2)[:, :, v * HOME:(v + 1) * HOME, :],
                                      sums[:, v, :, 0:HOME, :], carry[:, (v + 1) % 2, :, :, :], ALU.add).then_inc(summed, 1)
                    dve.wait_ge(summed, (n * 2 + j) * HOMES + (v + 1))
                    dve.memset(bank[2 * v + 1][:, 0:SLOTS * H], 0.0).then_inc(acc_free2, 1)

            dve.wait_ge(carry_zero, 1)
            with dve.Fori(0, TILES // 2) as i:
                tile_sums(0, i)
                tile_sums(1, i)
            tile_sums(0, TILES // 2)

            dve.sem_inc(y_free, 3)
            dve.wait_ge(bias_added, TILES)
            head_links, route_links, begin_links = 3 + INV_SQRT_LINKS, 11, 2
            per_tile = head_links + route_links + begin_links
            start = count[0]

            def linker(t, at):
                k = [at]

                def link_t(ins, nop_after=False):
                    k[0] += 1
                    ins.then_inc(dve_chain, 1)
                    dve.wait_ge(dve_chain, t * per_tile + (start + k[0]))
                    if nop_after:
                        dve.sem_inc(dve_mark, 1)
                link_t.count = k
                return link_t

            def normalise(j, t):
                l = linker(t, 0)
                s = small[j]
                dve.wait_ge(proj_done, t + 1)
                l(dve.scalar_tensor_tensor(y1[j][:, :].unsqueeze(1), bank[0][:, 0:D].unsqueeze(1), 1.0 / H,
                                           x_all[:, bass.ds(t, 1), :], ALU.mult, ALU.add))
                l(dve.bn_stats(s[:, 40:46], y1[j][:, :]), True)
                l(dve.bn_aggr(s[:, 46:48], s[:, 40:46]))
                inv_sqrt(l, s[:, 48:49], s[:, 47:48], s[:, 66:67], s[:, 67:68])
                dve.tensor_scalar(tn[j][:, :], y1[j][:, :], s[:, 46:47], s[:, 48:49], ALU.subtract, ALU.mult)\
                    .then_inc(tn_ready, 1)
                assert l.count[0] == head_links

            def route(j, t):
                l = linker(t, head_links)
                s = small[j]
                ex, probs, top, ids = s[:, 8:16], s[:, 16:24], s[:, 24:32], s[:, 32:34]
                dve.wait_ge(logit_done, t + 1)
                dve.tensor_reduce(s[:, 0:1], bank[1][:, D:D + NX], AX_X, ALU.max, negate=True).then_inc(shift_ready, 1)
                dve.wait_ge(exp_ready, t + 1)
                l(dve.reciprocal(s[:, 2:3], s[:, 1:2]))
                l(dve.tensor_scalar(probs, ex, s[:, 2:3], None, ALU.mult), True)
                l(dve.max(top, probs), True)
                l(dve.max_index(top_idx[j][:, :], top, probs))
                l(dve.tensor_copy(ids, top_idx[j][:, 0:2]))
                l(dve.tensor_tensor(s[:, 3:4], top[:, 0:1], top[:, 1:2], ALU.add))
                l(dve.tensor_scalar(s[:, 3:4], s[:, 3:4], 1e-12, None, ALU.max))
                l(dve.reciprocal(s[:, 4:5], s[:, 3:4]))
                l(dve.tensor_scalar(s[:, 50:58], expert_ids[:, :], ids[:, 0:1], s[:, 4:5], ALU.is_equal, ALU.mult))
                l(dve.tensor_scalar(s[:, 58:66], expert_ids[:, :], ids[:, 1:2], s[:, 4:5], ALU.is_equal, ALU.mult))
                l(dve.tensor_tensor(s[:, 50:58], s[:, 50:58], s[:, 58:66], ALU.add))
                dve.tensor_tensor(comb[j][:, :], s[:, 50:58], probs, ALU.mult).then_inc(comb_ready, 1)
                assert l.count[0] == head_links + route_links

            def begin(j, t, n):
                l = linker(t, head_links + route_links)
                dve.wait_ge(out_stored[j], n * 16)
                l(dve.tensor_tensor(res[j][:, :], y1[j][:, :], tn[j][:, :], ALU.add))
                dve.wait_ge(b2_done, t + 1)
                l(dve.tensor_tensor(res[j][:, :], res[j][:, :], bank[1][:, 0:D], ALU.add))

            def mix(j, t, e):
                dve.wait_ge(y_done, t * NX + (e + 1))
                dve.scalar_tensor_tensor(res[j][:, :], y_bank[e % 3][:, 0:D], comb[j][:, e:e + 1], res[j][:, :],
                                         ALU.mult, ALU.add).then_inc(y_free, 1)
                if e < NX - 1:
                    dve.wait_ge(y_free, t * NX + (e + 4))

            def tile(j, n, ahead):
                t = n * 2 + j
                if ahead:
                    normalise(1 - j, t + 1)
                for e in range(NX):
                    mix(j, t, e)
                    if ahead and e == 2:
                        route(1 - j, t + 1)
                if ahead:
                    begin(1 - j, t + 1, n + j)

            normalise(0, 0)
            route(0, 0)
            begin(0, 0, 0)
            with dve.Fori(0, TILES // 2) as i:
                tile(0, i, True)
                tile(1, i, True)
            tile(0, TILES // 2, False)


_INS = ['x', 'src', 'dst', 'L0_gnn_W', 'L0_gnn_att_src', 'L0_gnn_att_dst', 'L0_gnn_bias', 'L0_ffn_router_w',
        'L0_ffn_w1', 'L0_ffn_b1', 'L0_ffn_w2', 'L0_ffn_b2']


def kernel(**inputs):
    import numpy as _np
    import concourse.bacc as _bacc
    from concourse import mybir as _mybir
    from concourse.bass_utils import run_bass_kernel_spmd as _run

    nc = _bacc.Bacc("TRN2", target_bir_lowering=False, num_devices=1)
    arrays, args = {}, []
    for name in _INS:
        a = _np.ascontiguousarray(inputs[name])
        arrays[f"in_{name}"] = a
        args.append(nc.dram_tensor(f"in_{name}", a.shape, _mybir.dt.from_np(a.dtype), kind="ExternalInput").ap())
    args.append(nc.dram_tensor("out_0", inputs['x'].shape, _mybir.dt.float32, kind="ExternalOutput").ap())
    gat_moe_kernel(nc, *args)
    r = _run(nc, [arrays], core_ids=[0])
    return r.results[0]["out_0"]
```

```python
from contextlib import ExitStack

import concourse.bass as bass
from concourse import mybir

F32 = mybir.dt.float32
I32 = mybir.dt.int32
U32 = mybir.dt.uint32
U8 = mybir.dt.uint8
ALU = mybir.AluOpType
ACT = mybir.ActivationFunctionType
AX_X = mybir.AxisListType.X

P = 128
BIG = 1e30
LN_EPS = 1e-5
SOFTMAX_EPS = 1e-16
NEG_SLOPE = 0.2
RSQRT_MAGIC = float(0x5F3759DF)
NEWTON_STEPS = 3
STAGE2_LINKS = 8
INV_SQRT_LINKS = 4 + 3 * NEWTON_STEPS
CHUNKS = 16
HOME = 32
UNIT = 2
SPREAD = 20
OVER = SPREAD - UNIT
SLOTS = HOME + OVER
HOMES = P // HOME
G_RING = 16
HALF = 8
A_RING = 8
GROUP = 4
ACC_RING = 4
SCORE_LAG = 2
UNROLL = 5


def gat_moe_kernel(nc, x, src, dst, W, att_src, att_dst, gnn_bias, router_w, w1, b1, w2, b2, out):
    N, D = x.shape
    E = src.shape[0]
    H, C = att_src.shape
    NX = router_w.shape[0]
    TILES = -(-N // P)
    FULL = N // P
    LAST = N - FULL * P
    EC = E // CHUNKS
    BLK = P - 3
    KB = EC // BLK
    NB = E // BLK
    NS = TILES * HOMES
    assert EC * CHUNKS == E and KB * BLK == EC and H * CHUNKS == P and D == 2 * P
    assert D == 2 * P and C == D and NB % G_RING == 0 and TILES % UNROLL == 0 and KB % UNROLL == 0
    assert TILES % 2 == 1 and HOMES == ACC_RING and NS <= P and SLOTS * H <= 512 and HOME == 32

    BANK = 512 // (UNIT * H)
    MAX_PLACE = (ACC_RING - 1) * BANK + HOME // UNIT - 1
    assert MAX_PLACE < 128 and UNIT == 2 and BANK == 32
    ROW = D + H
    node_table = nc.dram_tensor("node_table", [TILES * P, ROW], F32).ap()
    edge_rows = nc.dram_tensor("edge_rows", [CHUNKS, KB, P, D], F32).ap()
    agg_table = nc.dram_tensor("agg_table", [TILES, P, 2 * H * P], F32).ap()

    with ExitStack() as ctx:
        def sb(name, shape, dt=F32):
            return ctx.enter_context(nc.sbuf_tensor(name, shape, dt))

        def sem(name):
            return ctx.enter_context(nc.semaphore(name))

        x_all = sb("x_all", [P, TILES, D])
        W_sb = sb("W_sb", [P, 2, H * C])
        expert_w = sb("expert_w", [P, 2, NX * 2 * D])
        w1_sb = expert_w[:, 0, :].rearrange("p (e k n) -> p e k n", e=NX, k=2)
        w2_sb = expert_w[:, 1, :].rearrange("p (e k n) -> p e k n", e=NX, k=2)
        lo_hot = expert_w[0:BLK, 0, 0:HALF * P].rearrange("p (c n) -> p c n", n=P)
        lo_hotT = [expert_w[:, 0, (1 + j) * HALF * P:(1 + j) * HALF * P + HALF * BLK] for j in range(2)]
        hi_picked = expert_w[0:BLK, 1, 0:HALF * TILES * H].rearrange("p (c n) -> p c n", c=HALF)
        hi_hot = expert_w[0:BLK, 1, 2048:2048 + HALF * TILES].rearrange("p (c n) -> p c n", c=HALF)
        stage1 = expert_w[:, :, :].rearrange("p a n -> p (a n)")
        xn = stage1[:, 0:TILES * D].rearrange("p (t d) -> p t d", d=D)
        reach_junk, first_home_bc, last_home_bc = (stage1[:, TILES * D + n * NB:TILES * D + (n + 1) * NB] for n in range(3))
        alpha = sb("alpha", [BLK, NB, H])
        dst_f = sb("dst_f", [BLK, NB])
        dst_rel = sb("dst_rel", [BLK, NB])
        src_k = sb("src_k", [P, KB + 1, CHUNKS], I32)
        dst_k = sb("dst_k", [BLK, KB + 1, CHUNKS], I32)
        dst_lo = sb("dst_lo", [BLK, KB + 1, CHUNKS])
        dst_hi = sb("dst_hi", [BLK, KB + 1, CHUNKS])
        dst_far = dst_f
        node_ids = sb("node_ids", [P, TILES * P])
        ident = sb("ident", [P, P])
        first_i = sb("first_i", [1, NB], I32)
        last_i = sb("last_i", [1, NB], I32)
        place = sb("place", [1, NB], I32)
        places = sb("places", [1, NB], U8)
        home = sb("home", [1, NB], I32)
        home_f = sb("home_f", [1, NB])
        extras = sb("extras", [1, NB], I32)
        extra_before = sb("extra_before", [1, NB + 1], I32)
        span_f = sb("span_f", [1, NB // GROUP])
        far_f = sb("far_f", [1, 2, NB // G_RING])
        far = sb("far", [1, NB // G_RING], I32)
        step_cols = sb("step_cols", [P, 4])
        steps_to = sb("steps_to", [1, P], I32)
        ones_row = sb("ones_row", [1, P])
        bias_bc = sb("bias_bc", [P, D])
        router_sb = sb("router_sb", [P, 2, NX])
        b1_sb = sb("b1_sb", [P, NX, 2])
        b2_sb = sb("b2_sb", [NX, D])
        va = sb("va", [P, 2, 2 * H])
        expert_ids = sb("expert_ids", [P, NX])
        home_ids = sb("home_ids", [P, 1])
        home_ids_i = sb("home_ids_i", [P, 1], I32)
        expert_ids_i = sb("expert_ids_i", [P, NX], I32)

        zeros = sb("zeros", [P, 1])
        chain_rows = sb("chain_rows", [1, 4 * P + 4])

        SC = EC + 2
        work = sb("work", [P, 5 * SC])
        edges_i = work[0:2 * CHUNKS, 0:EC].bitcast(I32)
        edges_f = work[0:2 * CHUNKS, SC:SC + EC]
        o = 3 * SC
        att_bc = work[:, o:o + 2 * H * C].rearrange("p (a n) -> p a n", a=2)
        o += 2 * H * C
        att_junk = work[:, o:o + C]
        o += C
        ids_i = work[:, o:o + TILES * P // 2].bitcast(I32)
        assert o + TILES * P // 2 <= 5 * SC
        o = TILES * D
        row_tmp = stage1[0:1, o:o + NB].bitcast(I32)
        first_f = stage1[0:1, o + NB:o + 2 * NB]
        last_home_f = stage1[0:1, o + 2 * NB:o + 3 * NB]
        extra_sum = stage1[0:1, o + 3 * NB:o + 4 * NB + 1]
        extra_f = chain_rows[0:1, 0:NB]
        buf_E = work[:, 0:EC]
        buf_keep = work[:, SC:SC + EC + 1]
        buf_reset = work[:, 2 * SC:2 * SC + EC + 1]
        o = 3 * HALF * P
        buf_F = stage1[:, o:o + EC]
        buf_B = work[:, 4 * SC:4 * SC + EC]
        dst_scan = work[:, 2 * SC:2 * SC + EC + 2].bitcast(I32)
        got_rows = [work[:, 3 * SC + j * HALF * ROW:3 * SC + (j + 1) * HALF * ROW].rearrange("p (s d) -> p s d", s=HALF)
                    for j in range(2)]
        pieces = [slice(n * (EC // UNROLL), (n + 1) * (EC // UNROLL)) for n in range(UNROLL)]
        o = 0
        spread = work[0:BLK, o:o + A_RING * SPREAD * H].rearrange("p (s n) -> p s n", s=A_RING)
        o += A_RING * SPREAD * H
        extra = work[0:BLK, o:o + 2 * HOME * H].rearrange("p (s n) -> p s n", s=2)
        o += 2 * HOME * H
        h_sb = [work[:, o + j * D:o + (j + 1) * D].rearrange("p (k n) -> p k n", k=2) for j in range(3)]
        assert o + 3 * D <= SC
        o = SC
        rows = work[:, o:o + G_RING * D].rearrange("p (s d) -> p s d", s=G_RING)
        o += G_RING * D
        assert o <= 3 * SC
        o = 3 * SC
        stage = [work[:, o + j * 2 * H * P:o + (j + 1) * 2 * H * P].rearrange("p (m n) -> p m n", n=P)
                 for j in range(2)]
        o += 4 * H * P
        aggt = [work[:, a:a + 2 * H * P].rearrange("p (m n) -> p m n", n=P) for a in (SC + G_RING * D, o)]
        assert SC + G_RING * D + 2 * H * P <= 3 * SC and o + 2 * H * P <= 5 * SC

        stats = sb("stats", [P, TILES, 6])
        mean = sb("mean", [P, TILES])
        rstd = sb("rstd", [P, TILES])
        half = sb("half", [P, TILES])
        inv_tmp = sb("inv_tmp", [P, TILES])
        ring1 = sb("ring1", [P, 2 * UNROLL * D])
        xnT = [ring1[:, j * D:(j + 1) * D] for j in range(UNROLL)]
        carry = ring1[:, 0:4 * HOME * H].rearrange("p (s k d h) -> p s k d h", s=2, k=2, h=H)
        o1 = 4 * HOME * H
        hot = ring1[0:BLK, o1:o1 + G_RING * SPREAD].rearrange("p (s d) -> p s d", s=G_RING)
        o1 += G_RING * SPREAD
        extra_hot = ring1[0:BLK, o1:o1 + HOME].unsqueeze(1)
        o1 += HOME
        tT = [ring1[:, o1 + j * D:o1 + (j + 1) * D].rearrange("p (k n) -> p k n", k=2) for j in range(2)]
        assert o1 + 2 * D + P <= 2 * UNROLL * D
        score_all = sb("score_all", [P, TILES, 2 * H])
        idx_stage = [sb(f"idx_stage{j}", [P, HALF], I32) for j in range(2)]
        edge_e = sb("edge_e", [BLK, P])
        edge_z = sb("edge_z", [BLK, HALF, H])
        score_d = [sb(f"score_d{j}", [BLK, HALF, H]) for j in range(2)]
        cols = sb("cols", [P, 8])

        y1 = [sb(f"y1_{j}", [P, D]) for j in range(2)]
        tn = [sb(f"tn{j}", [P, D]) for j in range(2)]
        res = [sb(f"res{j}", [P, D]) for j in range(2)]
        comb = [sb(f"comb{j}", [P, NX]) for j in range(2)]
        small = [sb(f"small{j}", [P, 80]) for j in range(2)]
        top_idx = [sb(f"top_idx{j}", [P, 8], U32) for j in range(2)]
        combT = ring1[0:NX, 2 * UNROLL * D - P:]

        banks = ctx.enter_context(nc.psum_tensor("banks", [P, 8, 512], F32))
        bank = [banks[:, j, :] for j in range(8)]
        alpha_bank = [bank[2], bank[3], bank[6], bank[7]]
        h_bank = [bank[2], bank[3], bank[5]]
        y_bank = [bank[6], bank[7], bank[4]]
        sums = banks[:, :, :].rearrange("p (k r) (d h) -> p r k d h", k=2, h=H)
        columns = banks[:, :, :].rearrange("p b n -> p (b n)")

        in_x, in_edges, in_att, in_W, in_weights, in_small, in_scan = (
            sem("in_x"), sem("in_edges"), sem("in_att"), sem("in_W"), sem("in_weights"), sem("in_small"), sem("in_scan"))
        in_ends = sem("in_ends")
        dve_chain, pool_chain = sem("dve_chain"), sem("pool_chain")
        dve_mark, pool_mark = sem("dve_mark"), sem("pool_mark")
        consts_ready = sem("consts_ready")
        x_pad = sem("x_pad")
        edges_ready = sem("edges_ready")
        edgesT_done, idx_ready = sem("edgesT_done"), sem("idx_ready")
        va_ready = sem("va_ready")
        xn_ready, xnT_done, xnT_ready, score_done, score_copied = (
            sem("xn_ready"), sem("xnT_done"), sem("xnT_ready"), sem("score_done"), sem("score_copied"))
        xn_stored = sem("xn_stored")
        tables_stored = sem("tables_stored")
        scan_pad = sem("scan_pad")
        idx_staged = sem("idx_staged")
        got = [sem(f"got{j}") for j in range(2)]
        rows_stored = [sem(f"rows_stored{j}") for j in range(2)]
        got_used = [sem(f"got_used{j}") for j in range(2)]
        lo_ready, loT_done, loT_ready = sem("lo_ready"), sem("loT_done"), sem("loT_ready")
        hi_done, hi_read = sem("hi_done"), sem("hi_read")
        edge_ready, edgeT_done, edge_copied = sem("edge_ready"), sem("edgeT_done"), sem("edge_copied")
        col_ready, row_done, row_ready, col_done = sem("col_ready"), sem("row_done"), sem("row_ready"), sem("col_done")
        exp_in, exp_out, scans_done = sem("exp_in"), sem("exp_out"), sem("scans_done")
        alpha_scan, alphaT_done, alpha_ready = sem("alpha_scan"), sem("alphaT_done"), sem("alpha_ready")
        home_row_ready, home_bc_done, step_cols_ready, step_row_done = (
            sem("home_row_ready"), sem("home_bc_done"), sem("step_cols_ready"), sem("step_row_done"))
        steps_ready = sem("steps_ready")
        rows_in = [sem(f"rows_in{j}") for j in range(G_RING // GROUP)]
        spread_ready, block_done, progress = sem("spread_ready"), sem("block_done"), sem("progress")
        diff_ready, hot_ready, extra_diff_ready = sem("diff_ready"), sem("hot_ready"), sem("extra_diff_ready")
        extra_hot_ready, extra_ready, extra_free = sem("extra_hot_ready"), sem("extra_ready"), sem("extra_free")
        carry_zero, carried0, carried1 = sem("carry_zero"), sem("carried0"), sem("carried1")
        summed0, summed1 = sem("summed0"), sem("summed1")
        acc_free, acc_free2 = sem("acc_free"), sem("acc_free2")
        stage_out = [sem(f"stage_out{j}") for j in range(2)]
        bias_added = sem("bias_added")
        agg_in = [sem(f"agg_in{j}") for j in range(2)]
        proj_done, tn_ready, tr_done, tT_ready = sem("proj_done"), sem("tn_ready"), sem("tr_done"), sem("tT_ready")
        logit_done, shift_ready, exp_ready = sem("logit_done"), sem("shift_ready"), sem("exp_ready")
        comb_ready, combT_done, combT_ready, b2_done = (
            sem("comb_ready"), sem("combT_done"), sem("combT_ready"), sem("b2_done"))
        hT_done, h_ready, y_done, y_free = sem("hT_done"), sem("h_ready"), sem("y_done"), sem("y_free")
        out_stored = [sem(f"out_stored{j}") for j in range(2)]

        scan_dst = dst.rearrange("(c j) -> c j", c=CHUNKS)
        block = ctx.enter_context(nc.Block())

        @block.sync
        def _(sp):
            sp.dma_start(edges_i[0:CHUNKS, :], src.rearrange("(c j) -> c j", c=CHUNKS)).then_inc(in_edges, 16)
            sp.dma_start(edges_i[CHUNKS:, :], scan_dst).then_inc(in_edges, 16)
            for row, at in ((first_i, 0), (last_i, BLK - 1)):
                sp.dma_start(row[:, :], dst.rearrange("(a b j) -> a b j", a=1, j=BLK)[:, :, at],
                             allow_slow_non_contiguous=True).then_inc(in_ends, 16)
            sp.wait_ge(x_pad, 1)
            sp.dma_start(x_all[:, 0:FULL, :], x[0:FULL * P, :].rearrange("(t p) d -> p t d", p=P)).then_inc(in_x, 16)
            sp.dma_start(x_all[0:LAST, FULL, :], x[FULL * P:N, :]).then_inc(in_x, 16)
            sp.dma_start(W_sb[:, :, :], W.rearrange("(k p) n -> p k n", p=P)).then_inc(in_W, 16)
            for a, att in enumerate((att_src, att_dst)):
                sp.dma_start(att_bc[:, a, :], att.rearrange("h c -> (h c)").partition_broadcast(P)).then_inc(in_att, 16)
            sp.dma_start(bias_bc[:, :], gnn_bias.partition_broadcast(P)).then_inc(in_small, 16)
            sp.dma_start(b2_sb[:, :], b2).then_inc(in_small, 16)
            for k in range(2):
                sp.dma_start(router_sb[:, k, :], router_w[:, k * P:(k + 1) * P].rearrange("e p -> p e"),
                             allow_slow_non_contiguous=True).then_inc(in_small, 16)
                sp.dma_start(b1_sb[:, :, k], b1[:, k * P:(k + 1) * P].rearrange("e p -> p e"),
                             allow_slow_non_contiguous=True).then_inc(in_small, 16)
            sp.wait_ge(scan_pad, 2)
            for h in range(H):
                r = h * CHUNKS
                sp.dma_start(dst_scan[r:r + CHUNKS, 1:EC + 1], scan_dst).then_inc(in_scan, 16)
                sp.dma_start(dst_scan[r + 1:r + CHUNKS, 0:1], scan_dst[0:CHUNKS - 1, EC - 1:EC],
                             allow_slow_non_contiguous=True).then_inc(in_scan, 16)
                sp.dma_start(dst_scan[r:r + CHUNKS - 1, EC + 1:EC + 2], scan_dst[1:CHUNKS, 0:1],
                             allow_slow_non_contiguous=True).then_inc(in_scan, 16)
            with sp.Fori(0, TILES // UNROLL) as i:
                sp.wait_ge(xn_ready, i * UNROLL + UNROLL)
                sp.dma_start(node_table[:, 0:D].rearrange("(t p) d -> p t d", p=P)[:, bass.ds(i * UNROLL, UNROLL), :],
                             xn[:, bass.ds(i * UNROLL, UNROLL), :]).then_inc(xn_stored, 16)
            sp.wait_ge(score_copied, TILES)
            sp.dma_start(node_table[:, D:].rearrange("(t p) h -> p t h", p=P), score_all[:, :, 0:H]).then_inc(tables_stored, 16)
            with sp.Fori(0, KB) as k:
                for j in range(2):
                    sp.wait_ge(got[j], k * (16 * HALF) + 16 * HALF)
                    sp.dma_start(edge_rows.rearrange("c k p d -> k p c d")[bass.ds(k, 1), :, j * HALF:(j + 1) * HALF, :]
                                 .rearrange("k p c d -> (k p) c d"), got_rows[j][:, :, 0:D]).then_inc(rows_stored[j], 16)
            for j in range(2):
                sp.wait_ge(rows_stored[j], 16 * KB)
            sp.wait_ge(scans_done, 1)
            blocks = edge_rows.rearrange("c k p d -> p (c k) d")
            for g in range(G_RING // GROUP):
                sp.dma_start(rows[:, g * GROUP:(g + 1) * GROUP, :], blocks[:, g * GROUP:(g + 1) * GROUP, :])\
                    .then_inc(rows_in[g], 16)
            sp.wait_ge(alpha_scan, UNROLL)
            for e in range(NX):
                sp.dma_start(w1_sb[:, e, :, :], w1[e].rearrange("(k p) n -> p k n", p=P)).then_inc(in_weights, 16)
                sp.dma_start(w2_sb[:, e, :, :], w2[e].rearrange("(k p) n -> p k n", p=P)).then_inc(in_weights, 16)
            with sp.Fori(0, NB // G_RING - 1) as i:
                for g in range(G_RING // GROUP):
                    sp.wait_ge(block_done, i * G_RING + (G_RING + (g + 1) * GROUP))
                    sp.dma_start(rows[:, g * GROUP:(g + 1) * GROUP, :],
                                 blocks[:, bass.ds(i * G_RING + (G_RING + g * GROUP), GROUP), :]).then_inc(rows_in[g], 16)

            def load_agg(j, n):
                sp.wait_ge(stage_out[j], (n + 1) * 16)
                sp.dma_start(aggt[j].rearrange("p m n -> p (m n)"),
                             agg_table[bass.ds(n * 2 + j, 1), :, :].rearrange("t p n -> (t p) n")).then_inc(agg_in[j], 16)

            def store_out(j, n):
                sp.wait_ge(y_free, (n * 2 + (j + 1)) * NX + 3)
                sp.dma_start(out[bass.ds((n * 2 + j) * P, P), :], res[j][:, :]).then_inc(out_stored[j], 16)

            load_agg(0, 0)
            load_agg(1, 0)
            with sp.Fori(0, TILES // 2 - 1) as i:
                for j in range(2):
                    sp.wait_ge(proj_done, i * 2 + (j + 1))
                    load_agg(j, i + 1)
                for j in range(2):
                    store_out(j, i)
            last = TILES // 2
            sp.wait_ge(proj_done, TILES - 2)
            load_agg(0, last)
            store_out(0, last - 1)
            store_out(1, last - 1)
            sp.wait_ge(y_free, TILES * NX + 3)
            sp.dma_start(out[FULL * P:N, :], res[0][0:LAST, :]).then_inc(out_stored[0], 16)
            sp.wait_ge(out_stored[0], 16 * (last + 1))
            sp.wait_ge(out_stored[1], 16 * last)

        @block.gpsimd
        def _(pool):
            count = [0]

            def link(ins):
                count[0] += 1
                ins.then_inc(pool_chain, 1)
                pool.wait_ge(pool_chain, count[0])

            pool.memset(x_all[:, FULL, :], 0.0).then_inc(x_pad, 1)
            pool.memset(dst_scan[:, 0:1], -1).then_inc(scan_pad, 1)
            pool.memset(dst_scan[:, EC + 1:EC + 2], -1).then_inc(scan_pad, 1)
            link(pool.memset(ident[:, :], 0.0))
            pool.affine_select(out=ident[:, :], in_=ident[:, :], compare_op=ALU.not_equal, fill=1.0, base=0,
                               pattern=[[-1, P]], channel_multiplier=1).then_inc(consts_ready, 1)
            link(pool.iota(expert_ids_i[:, :], pattern=[[1, NX]], base=0, channel_multiplier=0))
            pool.tensor_copy(expert_ids[:, :], expert_ids_i[:, :]).then_inc(consts_ready, 1)
            link(pool.iota(home_ids_i[:, :], pattern=[[0, 1]], base=0, channel_multiplier=1))
            pool.tensor_copy(home_ids[:, :], home_ids_i[:, :]).then_inc(consts_ready, 1)
            HALF_IDS = TILES * P // 2
            for n in range(2):
                link(pool.iota(ids_i[:, 0:HALF_IDS], pattern=[[1, HALF_IDS]], base=n * HALF_IDS, channel_multiplier=0))
                link(pool.tensor_copy(node_ids[:, n * HALF_IDS:(n + 1) * HALF_IDS], ids_i[:, 0:HALF_IDS]))
            pool.sem_inc(consts_ready, 1)

            pool.wait_ge(idx_ready, 1)
            pool.wait_ge(tables_stored, 16)
            pool.wait_ge(xn_stored, 16 * (TILES // UNROLL))
            pool.wait_ge(va_ready, 1)
            def stage_idx(k, j):
                pool.tensor_copy(idx_stage[j][:, :].unsqueeze(1), src_k[:, bass.ds(k, 1), j * HALF:(j + 1) * HALF])\
                    .then_inc(idx_staged, 1)

            stage_idx(0, 0)
            with pool.Fori(0, KB) as k:
                for j in range(2):
                    pool.wait_ge(rows_stored[j], k * 16)
                    pool.wait_ge(got_used[j], k)
                    pool.wait_ge(idx_staged, k * 2 + (j + 1))
                    pool.sem_inc(pool_mark, 1)
                    for c in range(HALF):
                        if c == HALF // 2:
                            pool.wait_ge(got[1 - j], (k + j) * (16 * HALF))
                            stage_idx(k + j, 1 - j)
                        pool.indirect_dma_start(got_rows[j][:, c, :], None, node_table,
                                                bass.IndirectOffsetOnAxis(idx_stage[j][:, c:c + 1], 0)).then_inc(got[j], 16)
            pool.wait_ge(in_small, 16 * 6)
            with pool.Fori(0, TILES) as t:
                pool.tensor_tensor(x_all[:, bass.ds(t, 1), :], x_all[:, bass.ds(t, 1), :], bias_bc[:, :].unsqueeze(1), ALU.add)\
                    .then_inc(bias_added, 1)

            pool.sem_inc(spread_ready, A_RING)

            def alphas(b, blocks, width):
                return alpha[:, bass.ds(b, blocks), :].unsqueeze(2).to_broadcast([BLK, blocks, width, H])

            def find(b, slot, blocks, spread_before):
                pool.wait_ge(spread_ready, spread_before + A_RING)
                pool.tensor_tensor(hot[:, slot:slot + blocks, :],
                                   node_ids[0:BLK, 0:SPREAD].unsqueeze(1).to_broadcast([BLK, blocks, SPREAD]),
                                   dst_rel[:, bass.ds(b, blocks)].unsqueeze(2).to_broadcast([BLK, blocks, SPREAD]),
                                   ALU.subtract).then_inc(diff_ready, blocks)
                pool.wait_ge(diff_ready, b + blocks)
                pool.sem_inc(pool_mark, 1)
                pool.tensor_single_scalar(hot[:, slot:slot + blocks, :], hot[:, slot:slot + blocks, :], 0.0,
                                          op=ALU.is_equal).then_inc(hot_ready, blocks)

            def spread_blocks(b, slot, blocks):
                at = pool.value_load(home[0:1, bass.ds(b + (blocks - 1), 1)], min_val=0, max_val=NS - 1)
                pool.wait_ge(alpha_ready, KB)
                pool.wait_ge(block_done, b + (blocks + G_RING - A_RING))
                pool.wait_ge(acc_free, at + 1)
                pool.wait_ge(acc_free2, at + 1)
                pool.wait_ge(hot_ready, b + blocks)
                to = slot % A_RING
                pool.tensor_tensor(
                    spread[:, to:to + blocks, :].rearrange("p s (d h) -> p s d h", h=H),
                    hot[:, slot:slot + blocks, :].unsqueeze(3).to_broadcast([BLK, blocks, SPREAD, H]),
                    alphas(b, blocks, SPREAD), ALU.mult).then_inc(spread_ready, blocks)
                return at

            with pool.Fori(0, NB // G_RING) as i:
                is_far = pool.value_load(far[0:1, bass.ds(i, 1)], min_val=0, max_val=2 * NS)
                with pool.If(is_far < 1):
                    find(i * G_RING, 0, G_RING, i * G_RING)
                    for slot in range(0, G_RING, GROUP):
                        spread_blocks(i * G_RING + slot, slot, GROUP)
                with pool.Else():
                    for slot in range(G_RING):
                        b = i * G_RING + slot
                        find(b, slot, 1, b)
                        at = spread_blocks(b, slot, 1)
                        more = pool.value_load(extras[0:1, bass.ds(b, 1)], min_val=0, max_val=NS)
                        before = pool.value_load(extra_before[0:1, bass.ds(b, 1)], min_val=0, max_val=NB + NS)
                        with pool.If(more > 0):
                            with pool.Fori(0, more) as d:
                                n = before + d
                                pool.wait_ge(extra_free, n + 1)
                                pool.wait_ge(extra_ready, n)
                                to = pool.snap((at + d) % NS)
                                pool.tensor_tensor(
                                    extra_hot, node_ids[0:BLK, bass.ds(to * HOME, HOME)].unsqueeze(1),
                                    dst_far[:, bass.ds(b, 1)].unsqueeze(2).to_broadcast([BLK, 1, HOME]),
                                    ALU.subtract).then_inc(extra_diff_ready, 1)
                                pool.wait_ge(extra_diff_ready, n + 1)
                                pool.sem_inc(pool_mark, 1)
                                pool.tensor_single_scalar(extra_hot, extra_hot, 0.0, op=ALU.is_equal)\
                                    .then_inc(extra_hot_ready, 1)
                                pool.wait_ge(extra_hot_ready, n + 1)
                                pool.wait_ge(acc_free, at + d + 1)
                                pool.wait_ge(acc_free2, at + d + 1)
                                pool.tensor_tensor(
                                    extra[:, bass.ds(n % 2, 1), :].rearrange("p o (d h) -> p o d h", h=H),
                                    extra_hot.unsqueeze(3).to_broadcast([BLK, 1, HOME, H]),
                                    alphas(b, 1, HOME), ALU.mult).then_inc(extra_ready, 1)

        @block.tensor
        def _(pe):
            pe.wait_ge(consts_ready, 2)
            pe.wait_ge(edges_ready, 1)
            for k in range(KB):
                m = pe.transpose(bank[k // 16][0:BLK, (k % 16) * 32:(k % 16) * 32 + 32],
                                 edges_f[:, k * BLK:(k + 1) * BLK], ident[0:32, 0:32])
            m.then_inc(edgesT_done, 1)
            for n in range(TILES + SCORE_LAG):
                if n == TILES - UNROLL:
                    pe.wait_ge(home_row_ready, 1)
                    for to, row in ((0, first_f), (1, home_f), (7, last_home_f)):
                        m = pe.matmul(bank[to][:, 0:NB], ones_row[0:1, :], row[0:1, :], start=True, stop=True)
                    m.then_inc(home_bc_done, 1)
                if n < TILES:
                    pe.wait_ge(xn_ready, n + 1)
                    if n >= UNROLL:
                        pe.wait_ge(score_copied, n + 1 - UNROLL)
                    pe.transpose(bank[2 + n % UNROLL][:, 0:P], xn[:, n, 0:P], ident[:, :])
                    pe.transpose(bank[2 + n % UNROLL][:, P:D], xn[:, n, P:D], ident[:, :]).then_inc(xnT_done, 1)
                s = n - SCORE_LAG
                if s == 0:
                    pe.wait_ge(va_ready, 1)
                if s >= 0:
                    pe.wait_ge(xnT_ready, s + 1)
                    for k in range(2):
                        m = pe.matmul(bank[2 + s % UNROLL][:, D:D + 2 * H], xnT[s % UNROLL][:, k * P:(k + 1) * P], va[:, k, :],
                                      start=(k == 0), stop=(k == 1))
                    m.then_inc(score_done, 1)
            pe.wait_ge(step_cols_ready, 1)
            pe.transpose(bank[1][0:1, 0:P], step_cols[:, 0:1], ident[:, :]).then_inc(step_row_done, 1)
            pe.wait_ge(steps_ready, 1)
            pe.wait_ge(score_copied, TILES)

            def turn_lo(j, n):
                pe.wait_ge(lo_ready, n + 1)
                pe.wait_ge(loT_ready, n)
                for c in range(HALF):
                    m = pe.transpose(bank[c // 4][:, (c % 4) * P:(c % 4) * P + BLK], lo_hot[:, c, :], ident[0:BLK, 0:BLK])
                m.then_inc(loT_done, 1)

            def pick_lo(j, n):
                pe.wait_ge(loT_ready, n + 1)
                pe.wait_ge(hi_read, n)
                for c in range(HALF):
                    m = pe.matmul(bank[2 + c // 2][0:BLK, (c % 2) * TILES * H:(c % 2 + 1) * TILES * H],
                                  lo_hotT[j][:, c * BLK:(c + 1) * BLK], score_all[:, :, H:2 * H], start=True, stop=True)
                m.then_inc(hi_done, 1)

            for j in range(2):
                turn_lo(j, j)
                pick_lo(j, j)
            with pe.Fori(0, KB) as k:
                for j in range(2):
                    turn_lo(j, k * 2 + (j + 2))
                    pick_lo(j, k * 2 + (j + 2))
                pe.wait_ge(edge_ready, k + 1)
                pe.wait_ge(edge_copied, k)
                pe.transpose(bank[7][:, 0:BLK], edge_e[:, :], ident[0:BLK, 0:BLK]).then_inc(edgeT_done, 1)
            for n in range(4):
                pe.wait_ge(col_ready, n + 1)
                pe.transpose(bank[0][0:1, 0:P], cols[:, 0:1], ident[:, :])
                pe.transpose(bank[0][0:1, P:2 * P], cols[:, 1:2], ident[:, :]).then_inc(row_done, 1)
                pe.wait_ge(row_ready, n + 1)
                pe.transpose(bank[1][:, 0:1], chain_rows[0:1, 3 * P + 1 + n % 2:4 * P + 1 + n % 2],
                             ident[0:1, 0:1]).then_inc(col_done, 1)
            for k in range(KB):
                if k % (KB // UNROLL) == 0:
                    pe.wait_ge(alpha_scan, k // (KB // UNROLL) + 1)
                if k >= 4:
                    pe.wait_ge(alpha_ready, k - 3)
                pe.transpose(alpha_bank[k % 4][0:BLK, 0:P], buf_E[:, k * BLK:(k + 1) * BLK], ident[:, :])\
                    .then_inc(alphaT_done, 1)

            pe.wait_ge(alpha_ready, KB)
            pe.sem_inc(block_done, G_RING - 1)
            pe.sem_inc(extra_free, 2)

            def add_block(at, slot):
                for k in range(2):
                    m = pe.matmul(columns[:, bass.ds(at * (UNIT * H) + k * ACC_RING * 512, SPREAD * H)],
                                  rows[0:BLK, slot, k * P:(k + 1) * P],
                                  spread[:, slot % A_RING, :],
                                  start=False, stop=True, skip_group_check=True)
                    m.then_inc(progress if k else block_done, 1)

            words = places[0:1, :].bitcast(I32)
            with pe.Fori(0, NB // G_RING) as i:
                is_far = pe.value_load(far[0:1, bass.ds(i, 1)], min_val=0, max_val=2 * NS)
                with pe.If(is_far < 1):
                    for g in range(G_RING // GROUP):
                        word = pe.value_load(words[0:1, bass.ds(i * (G_RING // GROUP) + g, 1)], min_val=0, max_val=2 ** 31 - 1)
                        pe.wait_ge(rows_in[g], i * 16 + 16)
                        pe.wait_ge(spread_ready, i * G_RING + ((g + 1) * GROUP + A_RING))
                        for s in range(GROUP):
                            add_block(nc.s_assert_within(
                                (word // 256 ** s) % 128, 0, MAX_PLACE,
                                skip_runtime_bounds_check_because="a byte of places is 32 * (home % 4) + less than 16"),
                                g * GROUP + s)
                with pe.Else():
                    for slot in range(G_RING):
                        b = i * G_RING + slot
                        if slot % GROUP == 0:
                            pe.wait_ge(rows_in[slot // GROUP], i * 16 + 16)
                        at = pe.value_load(place[0:1, bass.ds(b, 1)], min_val=0, max_val=MAX_PLACE)
                        pe.wait_ge(spread_ready, b + (1 + A_RING))
                        add_block(at, slot)
                        more = pe.value_load(extras[0:1, bass.ds(b, 1)], min_val=0, max_val=NS)
                        before = pe.value_load(extra_before[0:1, bass.ds(b, 1)], min_val=0, max_val=NB + NS)
                        start = pe.value_load(home[0:1, bass.ds(b, 1)], min_val=0, max_val=NS - 1)
                        with pe.If(more > 0):
                            with pe.Fori(0, more) as d:
                                n = before + d
                                pe.wait_ge(extra_ready, n + 1)
                                for k in range(2):
                                    m = pe.matmul(banks[:, bass.ds((start + d) % ACC_RING + k * ACC_RING, 1), 0:HOME * H],
                                                  rows[0:BLK, slot, k * P:(k + 1) * P], extra[:, bass.ds(n % 2, 1), :],
                                                  start=False, stop=True, skip_group_check=True)
                                m.then_inc(extra_free, 1)
                                pe.drain().then_inc(progress, 1)

            pe.wait_ge(acc_free, NS + 2)

            def project(j, n):
                pe.wait_ge(agg_in[j], (n + 1) * 16)
                for k in range(2):
                    for h in range(H):
                        m = pe.matmul(bank[0][:, 0:C], aggt[j][:, k * H + h, :], W_sb[:, k, h * C:(h + 1) * C],
                                      start=(k == 0 and h == 0), stop=(k == 1 and h == H - 1))
                m.then_inc(proj_done, 1)

            def turn_tn(j, t):
                pe.wait_ge(tn_ready, t + 1)
                for k in range(2):
                    m = pe.transpose(bank[1][:, k * P:(k + 1) * P], tn[j][:, k * P:(k + 1) * P], ident[:, :])
                m.then_inc(tr_done, 1)

            def router(j, t):
                pe.wait_ge(tT_ready, t + 1)
                for k in range(2):
                    m = pe.matmul(bank[1][:, D:D + NX], tT[j][:, k, :], router_sb[:, k, :], start=(k == 0), stop=(k == 1))
                m.then_inc(logit_done, 1)

            def turn_comb(j, t):
                pe.wait_ge(comb_ready, t + 1)
                pe.transpose(bank[1][0:NX, 384:384 + P], comb[j][:, :], ident[:, :]).then_inc(combT_done, 1)

            def bias_mix(t):
                pe.wait_ge(combT_ready, t + 1)
                pe.matmul(bank[1][:, 0:D], combT[:, :], b2_sb[:, :], start=True, stop=True).then_inc(b2_done, 1)

            def up(j, e):
                for f in range(2):
                    for k in range(2):
                        m = pe.matmul(h_bank[e % 3][:, f * P:(f + 1) * P], w1_sb[:, e, k, f * P:(f + 1) * P],
                                      tT[j][:, k, :], start=(k == 0), stop=(k == 1))
                m.then_inc(hT_done, 1)

            def down(j, e, t):
                pe.wait_ge(h_ready, t * NX + (e + 1))
                pe.wait_ge(y_free, t * NX + ((2, 3, 1)[e] if e < 3 else e + 1))
                for f in range(2):
                    m = pe.matmul(y_bank[e % 3][:, 0:D], h_sb[e % 3][:, f, :], w2_sb[:, e, f, :],
                                  start=(f == 0), stop=(f == 1))
                m.then_inc(y_done, 1)

            def tile(j, n, ahead, project_next):
                t = n * 2 + j
                for e in range(NX):
                    if ahead and e == 3:
                        turn_tn(1 - j, t + 1)
                    if e + 2 < NX:
                        up(j, e + 2)
                    if ahead and e == 3:
                        router(1 - j, t + 1)
                    down(j, e, t)
                    if ahead and e == NX - 2:
                        up(1 - j, 0)
                        turn_comb(1 - j, t + 1)
                if ahead:
                    bias_mix(t + 1)
                    up(1 - j, 1)
                if project_next:
                    project(j, n + 1)

            project(0, 0)
            turn_tn(0, 0)
            router(0, 0)
            project(1, 0)
            turn_comb(0, 0)
            bias_mix(0)
            pe.wait_ge(in_weights, 16 * 2 * NX)
            pe.wait_ge(acc_free, NS + ACC_RING)
            pe.wait_ge(acc_free2, NS + ACC_RING)
            up(0, 0)
            up(0, 1)
            with pe.Fori(0, TILES // 2 - 1) as i:
                tile(0, i, True, True)
                tile(1, i, True, True)
            tile(0, TILES // 2 - 1, True, True)
            tile(1, TILES // 2 - 1, True, False)
            tile(0, TILES // 2, False, False)

        @block.scalar
        def _(act):
            for n in range(TILES + SCORE_LAG):
                if n < TILES:
                    act.wait_ge(xnT_done, n + 1)
                    act.copy(xnT[n % UNROLL][:, :], bank[2 + n % UNROLL][:, 0:D]).then_inc(xnT_ready, 1)
                s = n - SCORE_LAG
                if s >= 0:
                    act.wait_ge(score_done, s + 1)
                    act.copy(score_all[:, s, :], bank[2 + s % UNROLL][:, D:D + 2 * H]).then_inc(score_copied, 1)
            def copy_lo(j, n):
                act.wait_ge(loT_done, n + 1)
                for q in range(2):
                    c = act.copy(lo_hotT[j][:, q * 4 * BLK:(q + 1) * 4 * BLK].rearrange("p (c n) -> p c n", c=4),
                                 bank[q].rearrange("p (c n) -> p c n", c=4)[:, :, 0:BLK])
                c.then_inc(loT_ready, 1)

            for j in range(2):
                copy_lo(j, j)
            with act.Fori(0, KB) as k:
                for j in range(2):
                    copy_lo(j, k * 2 + (j + 2))
                act.wait_ge(edgeT_done, k + 1)
                act.copy(buf_E[:, bass.ds(k * BLK, BLK)], bank[7][:, 0:BLK]).then_inc(edge_copied, 1)
            for n, piece in enumerate(pieces):
                act.wait_ge(exp_in, n + 1)
                act.activation(buf_E[:, piece], buf_E[:, piece], ACT.Exp).then_inc(exp_out, 1)
            alpha_v = alpha[:, :, :].rearrange("p (c k) h -> p k h c", k=KB)
            for k in range(KB):
                act.wait_ge(alphaT_done, k + 1)
                act.copy(alpha_v[:, k, :, :], alpha_bank[k % 4][0:BLK, 0:P].rearrange("p (h c) -> p h c", h=H))\
                    .then_inc(alpha_ready, 1)
            act.wait_ge(acc_free, ACC_RING)
            act.wait_ge(carry_zero, 1)

            def tile_out(j, n):
                for v in range(HOMES):
                    at = (n * 2 + j) * HOMES + v
                    last = act.value_load(steps_to[0:1, bass.ds(at, 1)], min_val=0, max_val=2 * NB + NS)
                    act.wait_ge(progress, last)
                    act.wait_ge(summed1, at)
                    act.copy(carry[:, v % 2, 1, 0:OVER, :], sums[:, v, 1, HOME:SLOTS, :]).then_inc(carried1, 1)
                    act.wait_ge(summed0, at + 1)
                    act.copy(carry[:, v % 2, 0, 0:OVER, :], sums[:, v, 0, HOME:SLOTS, :]).then_inc(carried0, 1)
                    act.wait_ge(carried0, at + 1)
                    act.copy(bank[v][:, 0:SLOTS * H], zeros[:, 0:1].to_broadcast([P, SLOTS * H])).then_inc(acc_free, 1)
                act.wait_ge(summed1, (n * 2 + j) * HOMES + HOMES)
                act.dma_start(agg_table[bass.ds(n * 2 + j, 1), :, :].rearrange("t p n -> (t p) n"),
                              stage[j].rearrange("p m n -> p (m n)")).then_inc(stage_out[j], 16)

            with act.Fori(0, TILES // 2) as i:
                tile_out(0, i)
                tile_out(1, i)
            tile_out(0, TILES // 2)

            act.wait_ge(in_small, 16 * 6)

            def turn(j, t):
                act.wait_ge(tr_done, t + 1)
                act.copy(tT[j][:, :, :], bank[1][:, 0:D].rearrange("p (k n) -> p k n", k=2)).then_inc(tT_ready, 1)

            def route(j, t):
                act.wait_ge(shift_ready, t + 1)
                act.activation(small[j][:, 8:8 + NX], bank[1][:, D:D + NX], ACT.Exp, bias=small[j][:, 0:1],
                               accum_out=small[j][:, 1:2]).then_inc(exp_ready, 1)

            def mix(t):
                act.wait_ge(combT_done, t + 1)
                act.copy(combT[:, :], bank[1][0:NX, 384:384 + P]).then_inc(combT_ready, 1)

            def gelus(e, t):
                act.wait_ge(hT_done, t * NX + (e + 1))
                for f in range(2):
                    g = act.activation(h_sb[e % 3][:, f, :], h_bank[e % 3][:, f * P:(f + 1) * P], ACT.Gelu,
                                       bias=b1_sb[:, e, f:f + 1])
                g.then_inc(h_ready, 1)

            def tile(j, n, ahead):
                t = n * 2 + j
                for e in range(NX):
                    gelus(e, t)
                    if ahead and e == 3:
                        turn(1 - j, t + 1)
                    if ahead and e == 4:
                        route(1 - j, t + 1)
                if ahead:
                    mix(t + 1)

            turn(0, 0)
            route(0, 0)
            mix(0)
            with act.Fori(0, TILES // 2) as i:
                tile(0, i, True)
                tile(1, i, True)
            tile(0, TILES // 2, False)

        @block.vector
        def _(dve):
            count = [0]

            def link(ins):
                count[0] += 1
                ins.then_inc(dve_chain, 1)
                dve.wait_ge(dve_chain, count[0])

            link(dve.memset(zeros[:, :], 0.0))
            def inv_sqrt(chained, y, var, t, half_v):
                chained(dve.tensor_scalar(half_v, var, LN_EPS, None, ALU.add))
                chained(dve.tensor_single_scalar(t.bitcast(I32), half_v.bitcast(I32), 1, op=ALU.arith_shift_right))
                chained(dve.tensor_scalar(y.bitcast(I32), t.bitcast(I32), -1.0, RSQRT_MAGIC, ALU.mult, ALU.add))
                chained(dve.tensor_scalar(half_v, half_v, -0.5, None, ALU.mult))
                for _ in range(NEWTON_STEPS):
                    chained(dve.tensor_tensor(t, y, y, ALU.mult))
                    chained(dve.tensor_tensor(t, t, half_v, ALU.mult))
                    chained(dve.scalar_tensor_tensor(y, t, 1.5, y, ALU.add, ALU.mult))

            link(dve.memset(ones_row[:, :], 1.0))
            link(dve.memset(src_k[:, :, :], 0))
            link(dve.memset(dst_k[:, :, :], 0))
            dve.wait_ge(in_edges, 32)
            dve.tensor_copy(edges_f, edges_i).then_inc(edges_ready, 1)
            dve.wait_ge(edgesT_done, 1)
            for n, (k0, k1) in enumerate(((0, 16), (16, KB))):
                v = bank[n][0:BLK, 0:(k1 - k0) * 32].rearrange("p (k c) -> p k c", c=32)
                link(dve.tensor_copy(dst_f[:, :].rearrange("p (c k) -> p k c", k=KB)[:, k0:k1, :], v[:, :, CHUNKS:]))
                link(dve.tensor_copy(dst_k[:, k0:k1, :], v[:, :, CHUNKS:]))
                link(dve.tensor_copy(src_k[0:BLK, k0:k1, :], v[:, :, 0:CHUNKS]))
            dve.sem_inc(idx_ready, 1)
            link(dve.tensor_single_scalar(dst_hi[:, :, :].bitcast(I32), dst_k[:, :, :], 7, op=ALU.arith_shift_right))
            link(dve.tensor_single_scalar(dst_k[:, :, :], dst_k[:, :, :], P - 1, op=ALU.bitwise_and))
            link(dve.tensor_copy(dst_lo[:, :, :], dst_k[:, :, :]))
            link(dve.tensor_copy(dst_k[:, :, :], dst_hi[:, :, :].bitcast(I32)))
            link(dve.tensor_copy(dst_hi[:, :, :], dst_k[:, :, :]))
            dve.wait_ge(in_x, 32)
            with dve.Fori(0, TILES // UNROLL) as i:
                for j in range(UNROLL):
                    dve.bn_stats(stats[:, bass.ds(i * UNROLL + j, 1), :].rearrange("p t s -> p (t s)"),
                                 x_all[:, bass.ds(i * UNROLL + j, 1), :].rearrange("p t d -> p (t d)")).then_inc(dve_chain, 1)
            count[0] += TILES
            dve.wait_ge(dve_chain, count[0])
            link(dve.tensor_tensor(mean[:, :], stats[:, :, 1], stats[:, :, 4], ALU.add))
            link(dve.tensor_scalar(mean[:, :], mean[:, :], 0.5, None, ALU.mult))
            link(dve.tensor_tensor(half[:, :], stats[:, :, 1], stats[:, :, 4], ALU.subtract))
            link(dve.tensor_scalar(half[:, :], half[:, :], 0.5, None, ALU.mult))
            link(dve.tensor_tensor(half[:, :], half[:, :], half[:, :], ALU.mult))
            link(dve.tensor_tensor(rstd[:, :], stats[:, :, 2], stats[:, :, 5], ALU.add))
            link(dve.scalar_tensor_tensor(rstd[:, :], rstd[:, :], 1.0 / D, half[:, :], ALU.mult, ALU.add))
            inv_sqrt(link, rstd[:, :], rstd[:, :], half[:, :], inv_tmp[:, :])
            dve.wait_ge(in_att, 32)
            dve.wait_ge(in_W, 16)
            for a in range(2):
                for k in range(2):
                    for h in range(H):
                        link(dve.tensor_tensor_reduce(out=att_junk, in0=W_sb[:, k, h * C:(h + 1) * C],
                                                      in1=att_bc[:, a, h * C:(h + 1) * C], scale=1.0, scalar=0.0,
                                                      op0=ALU.mult, op1=ALU.add,
                                                      accum_out=va[:, k, a * H + h:a * H + h + 1]))
            dve.sem_inc(va_ready, 1)
            with dve.Fori(0, TILES // UNROLL) as i:
                for j in range(UNROLL):
                    t = i * UNROLL + j
                    dve.tensor_scalar(xn[:, bass.ds(t, 1), :], x_all[:, bass.ds(t, 1), :], mean[:, bass.ds(t, 1)],
                                      rstd[:, bass.ds(t, 1)], ALU.subtract, ALU.mult).then_inc(xn_ready, 1)
            dve.wait_ge(in_ends, 32)
            link(dve.tensor_single_scalar(row_tmp[:, :], first_i[:, :], ACC_RING * HOME - 1, op=ALU.bitwise_and))
            link(dve.tensor_single_scalar(row_tmp[:, :], row_tmp[:, :], 1, op=ALU.arith_shift_right))
            link(dve.tensor_single_scalar(place[:, :], row_tmp[:, :], (ACC_RING - 1) * (HOME // UNIT), op=ALU.bitwise_and))
            link(dve.scalar_tensor_tensor(place[:, :], place[:, :], float(BANK // (HOME // UNIT) - 1), row_tmp[:, :],
                                          ALU.mult, ALU.add))
            link(dve.tensor_copy(places[:, :], place[:, :]))
            link(dve.tensor_single_scalar(home[:, :], first_i[:, :], 5, op=ALU.arith_shift_right))
            link(dve.tensor_copy(home_f[:, :], home[:, :]))
            link(dve.tensor_single_scalar(row_tmp[:, :], last_i[:, :], 5, op=ALU.arith_shift_right))
            link(dve.tensor_copy(last_home_f[:, :], row_tmp[:, :]))
            link(dve.tensor_single_scalar(row_tmp[:, :], first_i[:, :], -UNIT, op=ALU.bitwise_and))
            link(dve.tensor_copy(first_f[:, :], row_tmp[:, :]))
            link(dve.tensor_copy(extra_f[:, :], last_i[:, :]))
            link(dve.tensor_tensor(extra_f[:, :], extra_f[:, :], first_f[:, :], ALU.subtract))
            link(dve.tensor_scalar(extra_f[:, :], extra_f[:, :], float(SPREAD), None, ALU.is_ge))
            link(dve.tensor_tensor(last_home_f[:, :], last_home_f[:, :], home_f[:, :], ALU.subtract))
            link(dve.scalar_tensor_tensor(extra_f[:, :], last_home_f[:, :], 1.0, extra_f[:, :], ALU.add, ALU.mult))
            link(dve.scalar_tensor_tensor(last_home_f[:, :], extra_f[:, :], -1.0, home_f[:, :], ALU.add, ALU.add))
            dve.sem_inc(home_row_ready, 1)
            link(dve.tensor_copy(extras[:, :], extra_f[:, :]))
            link(dve.memset(extra_sum[:, 0:1], 0.0))
            link(dve.tensor_tensor_scan(extra_sum[:, 1:NB + 1], extra_f[:, :], extra_f[:, :], 0.0, ALU.add, ALU.bypass))
            link(dve.tensor_copy(extra_before[:, :], extra_sum[:, :]))
            homes_g = home_f[:, :].rearrange("p (g b) -> p g b", b=GROUP)
            link(dve.tensor_tensor(span_f[:, :], homes_g[:, :, GROUP - 1], homes_g[:, :, 0], ALU.subtract))
            link(dve.tensor_scalar(span_f[:, :], span_f[:, :], float(ACC_RING), None, ALU.is_ge))
            link(dve.tensor_reduce(far_f[:, 0, :], span_f[:, :].rearrange("p (i g) -> p i g", g=G_RING // GROUP), AX_X, ALU.max))
            link(dve.tensor_reduce(far_f[:, 1, :], extra_f[:, :].rearrange("p (i b) -> p i b", b=G_RING), AX_X, ALU.max))
            link(dve.tensor_tensor(far_f[:, 0, :], far_f[:, 0, :], far_f[:, 1, :], ALU.add))
            link(dve.tensor_copy(far[:, :], far_f[:, 0, :]))
            dve.wait_ge(consts_ready, 3)
            dve.wait_ge(home_bc_done, 1)
            link(dve.scalar_tensor_tensor(dst_rel[:, :], bank[0][0:BLK, 0:NB], -1.0, dst_f[:, :], ALU.mult, ALU.add))
            link(dve.tensor_scalar(reach_junk[0:BLK, :], dst_rel[:, :], float(SPREAD), None, ALU.is_ge))
            link(dve.scalar_tensor_tensor(dst_far[:, :], dst_f[:, :], 1.0, reach_junk[0:BLK, :], ALU.add, ALU.mult))
            link(dve.tensor_scalar(dst_far[:, :], dst_far[:, :], 1.0, None, ALU.subtract))
            link(dve.tensor_copy(first_home_bc, bank[1][:, 0:NB]))
            link(dve.tensor_copy(last_home_bc, bank[7][:, 0:NB]))
            link(dve.tensor_scalar(reach_junk, first_home_bc, home_ids[:, 0:1], None, ALU.is_le))
            link(dve.tensor_reduce(step_cols[:, 0:1], reach_junk, AX_X, ALU.add))
            link(dve.scalar_tensor_tensor(reach_junk, last_home_bc, home_ids[:, 0:1], first_home_bc, ALU.min, ALU.subtract))
            link(dve.tensor_scalar(reach_junk, reach_junk, 1.0, 0.0, ALU.add, ALU.max))
            link(dve.tensor_reduce(step_cols[:, 1:2], reach_junk, AX_X, ALU.add))
            link(dve.tensor_tensor(step_cols[:, 0:1], step_cols[:, 0:1], step_cols[:, 1:2], ALU.add))
            dve.sem_inc(step_cols_ready, 1)
            dve.wait_ge(step_row_done, 1)
            dve.tensor_copy(steps_to[:, :], bank[1][0:1, 0:P]).then_inc(steps_ready, 1)
            dve.wait_ge(in_scan, 16 * 3 * H)
            link(dve.tensor_tensor(cols[:, 2:4], dst_scan[:, 0:2], dst_scan[:, EC:EC + 2], ALU.is_equal))
            link(dve.tensor_scalar(cols[:, 4:6], cols[:, 2:4], 1.0, BIG, ALU.subtract, ALU.mult))
            dve.wait_ge(xn_stored, 16 * (TILES // UNROLL))
            dve.wait_ge(xnT_done, TILES)
            dve.wait_ge(consts_ready, 4)
            def one_hot_lo(k, j, n):
                dve.wait_ge(loT_done, n)
                dve.tensor_tensor(lo_hot[:, :, :], node_ids[0:BLK, 0:P].unsqueeze(1).to_broadcast([BLK, HALF, P]),
                                  dst_lo[:, bass.ds(k, 1), j * HALF:(j + 1) * HALF].rearrange("p o c -> p (o c)")
                                  .unsqueeze(2).to_broadcast([BLK, HALF, P]), ALU.is_equal).then_inc(lo_ready, 1)

            def pick_hi(k, j, l):
                l(dve.tensor_tensor(hi_hot[:, :, :], node_ids[0:BLK, 0:TILES].unsqueeze(1).to_broadcast([BLK, HALF, TILES]),
                                    dst_hi[:, bass.ds(k, 1), j * HALF:(j + 1) * HALF].rearrange("p o c -> p (o c)")
                                    .unsqueeze(2).to_broadcast([BLK, HALF, TILES]), ALU.is_equal))
                dve.wait_ge(hi_done, k * 2 + (j + 1))
                for q in range(HALF // 2):
                    m = dve.tensor_tensor(
                        hi_picked[:, 2 * q:2 * q + 2, :].rearrange("p c (t h) -> p c t h", h=H),
                        bank[2 + q][0:BLK, 0:2 * TILES * H].rearrange("p (c t h) -> p c t h", c=2, h=H),
                        hi_hot[:, 2 * q:2 * q + 2, :].unsqueeze(3).to_broadcast([BLK, 2, TILES, H]), ALU.mult)
                m.then_inc(hi_read, 1)
                dve.wait_ge(hi_read, k * 2 + (j + 1))
                l(dve.tensor_reduce(score_d[j][:, :, :], hi_picked[:, :, :].rearrange("p c (t h) -> p c h t", h=H),
                                    AX_X, ALU.add))

            def edge_score(k, j, l):
                dve.wait_ge(got[j], k * (16 * HALF) + 16 * HALF)
                dve.tensor_tensor(edge_z[:, :, :], got_rows[j][0:BLK, :, D:ROW], score_d[j][:, :, :], ALU.add)\
                    .then_inc(got_used[j], 1)
                dve.wait_ge(got_used[j], k + 1)
                if j == 0:
                    dve.wait_ge(edgeT_done, k)
                l(dve.scalar_tensor_tensor(
                    edge_e[:, :].rearrange("p (h c) -> p c h", h=H)[:, j * HALF:(j + 1) * HALF, :], edge_z[:, :, :],
                    NEG_SLOPE, edge_z[:, :, :], ALU.mult, ALU.max))

            one_hot_lo(0, 0, 0)
            one_hot_lo(0, 1, 1)
            pick_hi(0, 0, link)
            base = count[0]
            with dve.Fori(0, KB) as k:
                at = [0]

                def link_k(ins):
                    at[0] += 1
                    ins.then_inc(dve_chain, 1)
                    dve.wait_ge(dve_chain, k * STAGE2_LINKS + (base + at[0]))

                one_hot_lo(k + 1, 0, k * 2 + 2)
                pick_hi(k, 1, link_k)
                edge_score(k, 0, link_k)
                one_hot_lo(k + 1, 1, k * 2 + 3)
                pick_hi(k + 1, 0, link_k)
                edge_score(k, 1, link_k)
                at_k = bass.ds(k * BLK, BLK)
                link_k(dve.tensor_tensor(buf_keep[:, at_k], dst_scan[:, at_k], dst_scan[:, bass.ds(k * BLK + 1, BLK)],
                                         ALU.is_equal))
                link_k(dve.tensor_scalar(buf_reset[:, at_k], buf_keep[:, at_k], 1.0, BIG, ALU.subtract, ALU.mult))
                dve.sem_inc(edge_ready, 1)
                assert at[0] == STAGE2_LINKS
            count[0] += KB * STAGE2_LINKS
            link(dve.tensor_tensor(buf_keep[:, EC:EC + 1], dst_scan[:, EC:EC + 1], dst_scan[:, EC + 1:EC + 2], ALU.is_equal))
            link(dve.tensor_scalar(buf_reset[:, EC:EC + 1], buf_keep[:, EC:EC + 1], 1.0, BIG, ALU.subtract, ALU.mult))
            dve.wait_ge(edge_copied, KB)

            turn = [0]

            def chained_scan(res_v, data0, data1, all_keep, op0, op1, init, back):
                n = turn[0]
                turn[0] += 1
                r = (lambda a: a[:, ::-1]) if back else (lambda a: a)
                end = res_v[:, 0:1] if back else res_v[:, EC - 1:EC]
                link(dve.tensor_tensor_scan(r(res_v), r(data0), r(data1), init, op0, op1))
                link(dve.tensor_copy(cols[:, 1:2], all_keep))
                dve.tensor_copy(cols[:, 0:1], end).then_inc(col_ready, 1)
                dve.wait_ge(row_done, n + 1)
                link(dve.tensor_copy(chain_rows[0:1, 0:2 * P], bank[0][0:1, 0:2 * P]))
                vals, keeps = chain_rows[0:1, 0:P], chain_rows[0:1, P:2 * P]
                shifted = chain_rows[0:1, 3 * P + 1 + n % 2:4 * P + 1 + n % 2]
                link(dve.memset(chain_rows[0:1, 3 * P:4 * P + 4], init))
                outs = chain_rows[0:1, 2 * P:3 * P]
                link(dve.tensor_tensor_scan(r(outs), r(keeps), r(vals), init, op0, op1))
                if back:
                    dve.tensor_copy(shifted[:, 0:P - 1], outs[:, 1:P]).then_inc(row_ready, 1)
                else:
                    dve.tensor_copy(shifted[:, 1:P], outs[:, 0:P - 1]).then_inc(row_ready, 1)
                dve.wait_ge(col_done, n + 1)
                link(dve.tensor_copy(cols[:, 6:7], bank[1][:, 0:1]))
                link(dve.tensor_tensor_scan(r(res_v), r(data0), r(data1), cols[:, 6:7], op0, op1))

            chained_scan(buf_F, buf_reset[:, 0:EC], buf_E, cols[:, 4:5], ALU.add, ALU.max, -BIG, False)
            for j in range(2):
                dve.wait_ge(rows_stored[j], 16 * KB)
            chained_scan(buf_B, buf_reset[:, 1:EC + 1], buf_F, cols[:, 5:6], ALU.add, ALU.max, -BIG, True)
            for piece in pieces:
                dve.tensor_tensor(buf_E[:, piece], buf_E[:, piece], buf_B[:, piece], ALU.subtract).then_inc(exp_in, 1)
            dve.wait_ge(exp_out, UNROLL)
            chained_scan(buf_F, buf_keep[:, 0:EC], buf_E, cols[:, 2:3], ALU.mult, ALU.add, 0.0, False)
            chained_scan(buf_B, buf_keep[:, 1:EC + 1], buf_E, cols[:, 3:4], ALU.mult, ALU.add, 0.0, True)
            dve.sem_inc(scans_done, 1)
            link(dve.tensor_tensor(buf_B, buf_B, buf_E, ALU.subtract))
            link(dve.scalar_tensor_tensor(buf_F, buf_F, SOFTMAX_EPS, buf_B, ALU.add, ALU.add))
            for piece in pieces:
                link(dve.reciprocal(buf_F[:, piece], buf_F[:, piece]))
                dve.tensor_tensor(buf_E[:, piece], buf_E[:, piece], buf_F[:, piece], ALU.mult).then_inc(alpha_scan, 1)

            dve.memset(ring1[:, 0:4 * HOME * H], 0.0).then_inc(carry_zero, 1)
            for r in range(ACC_RING):
                if r == 2:
                    dve.wait_ge(alpha_ready, KB)
                dve.memset(bank[r][:, :], 0.0).then_inc(acc_free, 1)
                dve.memset(bank[ACC_RING + r][:, :], 0.0).then_inc(acc_free2, 1)

            def tile_sums(j, n):
                dve.wait_ge(stage_out[j], n * 16)
                for v in range(HOMES):
                    at = (n * 2 + j) * HOMES + v
                    last = dve.value_load(steps_to[0:1, bass.ds(at, 1)], min_val=0, max_val=2 * NB + NS)
                    dve.wait_ge(progress, last)
                    for k, carried, summed in ((0, carried0, summed0), (1, carried1, summed1)):
                        dve.wait_ge(carried, at + k)
                        dve.tensor_tensor(stage[j].rearrange("p (k h) n -> p k n h", k=2)[:, k, v * HOME:(v + 1) * HOME, :],
                                          sums[:, v, k, 0:HOME, :], carry[:, (v + 1) % 2, k, :, :], ALU.add).then_inc(summed, 1)
                    dve.wait_ge(summed1, at + 1)
                    dve.memset(bank[ACC_RING + v][:, 0:SLOTS * H], 0.0).then_inc(acc_free2, 1)

            dve.wait_ge(carry_zero, 1)
            with dve.Fori(0, TILES // 2) as i:
                tile_sums(0, i)
                tile_sums(1, i)
            tile_sums(0, TILES // 2)

            dve.sem_inc(y_free, 3)
            dve.wait_ge(bias_added, TILES)
            head_links, route_links, begin_links = 3 + INV_SQRT_LINKS, 11, 2
            per_tile = head_links + route_links + begin_links
            start = count[0]

            def linker(t, at):
                k = [at]

                def link_t(ins, nop_after=False):
                    k[0] += 1
                    ins.then_inc(dve_chain, 1)
                    dve.wait_ge(dve_chain, t * per_tile + (start + k[0]))
                    if nop_after:
                        dve.sem_inc(dve_mark, 1)
                link_t.count = k
                return link_t

            def normalise(j, t):
                l = linker(t, 0)
                s = small[j]
                dve.wait_ge(proj_done, t + 1)
                l(dve.scalar_tensor_tensor(y1[j][:, :].unsqueeze(1), bank[0][:, 0:D].unsqueeze(1), 1.0 / H,
                                           x_all[:, bass.ds(t, 1), :], ALU.mult, ALU.add))
                l(dve.bn_stats(s[:, 40:46], y1[j][:, :]), True)
                l(dve.bn_aggr(s[:, 46:48], s[:, 40:46]))
                inv_sqrt(l, s[:, 48:49], s[:, 47:48], s[:, 66:67], s[:, 67:68])
                dve.tensor_scalar(tn[j][:, :], y1[j][:, :], s[:, 46:47], s[:, 48:49], ALU.subtract, ALU.mult)\
                    .then_inc(tn_ready, 1)
                assert l.count[0] == head_links

            def route(j, t):
                l = linker(t, head_links)
                s = small[j]
                ex, probs, top, ids = s[:, 8:16], s[:, 16:24], s[:, 24:32], s[:, 32:34]
                dve.wait_ge(logit_done, t + 1)
                dve.tensor_reduce(s[:, 0:1], bank[1][:, D:D + NX], AX_X, ALU.max, negate=True).then_inc(shift_ready, 1)
                dve.wait_ge(exp_ready, t + 1)
                l(dve.reciprocal(s[:, 2:3], s[:, 1:2]))
                l(dve.tensor_scalar(probs, ex, s[:, 2:3], None, ALU.mult), True)
                l(dve.max(top, probs), True)
                l(dve.max_index(top_idx[j][:, :], top, probs))
                l(dve.tensor_copy(ids, top_idx[j][:, 0:2]))
                l(dve.tensor_tensor(s[:, 3:4], top[:, 0:1], top[:, 1:2], ALU.add))
                l(dve.tensor_scalar(s[:, 3:4], s[:, 3:4], 1e-12, None, ALU.max))
                l(dve.reciprocal(s[:, 4:5], s[:, 3:4]))
                l(dve.tensor_scalar(s[:, 50:58], expert_ids[:, :], ids[:, 0:1], s[:, 4:5], ALU.is_equal, ALU.mult))
                l(dve.tensor_scalar(s[:, 58:66], expert_ids[:, :], ids[:, 1:2], s[:, 4:5], ALU.is_equal, ALU.mult))
                l(dve.tensor_tensor(s[:, 50:58], s[:, 50:58], s[:, 58:66], ALU.add))
                dve.tensor_tensor(comb[j][:, :], s[:, 50:58], probs, ALU.mult).then_inc(comb_ready, 1)
                assert l.count[0] == head_links + route_links

            def begin(j, t, n):
                l = linker(t, head_links + route_links)
                dve.wait_ge(out_stored[j], n * 16)
                l(dve.tensor_tensor(res[j][:, :], y1[j][:, :], tn[j][:, :], ALU.add))
                dve.wait_ge(b2_done, t + 1)
                l(dve.tensor_tensor(res[j][:, :], res[j][:, :], bank[1][:, 0:D], ALU.add))

            def mix(j, t, e):
                dve.wait_ge(y_done, t * NX + (e + 1))
                dve.scalar_tensor_tensor(res[j][:, :], y_bank[e % 3][:, 0:D], comb[j][:, e:e + 1], res[j][:, :],
                                         ALU.mult, ALU.add).then_inc(y_free, 1)
                if e < NX - 1:
                    dve.wait_ge(y_free, t * NX + (e + 4))

            def tile(j, n, ahead):
                t = n * 2 + j
                if ahead:
                    normalise(1 - j, t + 1)
                for e in range(NX):
                    mix(j, t, e)
                    if ahead and e == 2:
                        route(1 - j, t + 1)
                if ahead:
                    begin(1 - j, t + 1, n + j)

            normalise(0, 0)
            route(0, 0)
            begin(0, 0, 0)
            with dve.Fori(0, TILES // 2) as i:
                tile(0, i, True)
                tile(1, i, True)
            tile(0, TILES // 2, False)


_INS = ['x', 'src', 'dst', 'L0_gnn_W', 'L0_gnn_att_src', 'L0_gnn_att_dst', 'L0_gnn_bias', 'L0_ffn_router_w',
        'L0_ffn_w1', 'L0_ffn_b1', 'L0_ffn_w2', 'L0_ffn_b2']


def kernel(**inputs):
    import numpy as _np
    import concourse.bacc as _bacc
    from concourse import mybir as _mybir
    from concourse.bass_utils import run_bass_kernel_spmd as _run

    nc = _bacc.Bacc("TRN2", target_bir_lowering=False, num_devices=1)
    arrays, args = {}, []
    for name in _INS:
        a = _np.ascontiguousarray(inputs[name])
        arrays[f"in_{name}"] = a
        args.append(nc.dram_tensor(f"in_{name}", a.shape, _mybir.dt.from_np(a.dtype), kind="ExternalInput").ap())
    args.append(nc.dram_tensor("out_0", inputs['x'].shape, _mybir.dt.float32, kind="ExternalOutput").ap())
    gat_moe_kernel(nc, *args)
    r = _run(nc, [arrays], core_ids=[0])
    return r.results[0]["out_0"]
```
